# Optimizing a Trainium2 kernel written in Bass

```python
import numpy as np
import jax
import jax.numpy as jnp

def _softmax(x, axis=-1):
    return jax.nn.softmax(x, axis=axis)

def _gelu(x):
    return jax.nn.gelu(x, approximate=True)

def _silu(x):
    return jax.nn.silu(x)

def _sigmoid(x):
    return jax.nn.sigmoid(x)

def _layernorm(x, axis=-1, eps=1e-05):
    m = jnp.mean(x, axis=axis, keepdims=True)
    v = jnp.var(x, axis=axis, keepdims=True)
    return (x - m) / jnp.sqrt(v + eps)

def _scatter_add(tgt, idx, src, axis=0):
    return tgt.at[idx].add(src)

def _segment_sum(src, seg, n):
    return jax.ops.segment_sum(src, seg, n)
kernel_name = 'mk_seq_postln_d1_jaxref_r8_235fc1'

def setup_inputs(seed: int=0):
    np.random.seed(seed)
    _w = jnp.asarray

    def _L0_attn_setup():
        import jax, jax.numpy as jnp
        import numpy as np
        B, N, D, H = (4, 256, 128, 8)
        HD = D // H
        TEMPER = 1.0
        LN_EPS = 1e-05

        def _leaky(x):
            return jnp.where(x > 0, x, 0.01 * x)
        key = jax.random.key(seed)
        ks = jax.random.split(key, 6)
        return {'h': jax.random.normal(ks[0], (B, N, D), dtype=jnp.float32), 'Wl': jax.random.normal(ks[1], (D, D), dtype=jnp.float32) * D ** (-0.5), 'Wr': jax.random.normal(ks[2], (D, D), dtype=jnp.float32) * D ** (-0.5), 'att_l': jax.random.normal(ks[3], (1, HD), dtype=jnp.float32) * HD ** (-0.5), 'att_r': jax.random.normal(ks[4], (1, HD), dtype=jnp.float32) * HD ** (-0.5), 'Wf': jax.random.normal(ks[5], (D, D), dtype=jnp.float32) * D ** (-0.5), 'ln_gamma': jnp.ones((D,), dtype=jnp.float32), 'ln_beta': jnp.zeros((D,), dtype=jnp.float32)}
    _L0_attn_in = _L0_attn_setup()

    def _L0_ffn_setup():
        import jax, jax.numpy as jnp
        import numpy as np
        D_MODEL = 128
        D_HIDDEN = 512
        NUM_BANKS = 16
        NUM_SELECTED = 2
        key = jax.random.key(seed)
        ks = jax.random.split(key, 7)
        s = 0.02
        return {'tensor': jax.random.normal(ks[0], (4, 128, D_MODEL), dtype=jnp.float32), 'Wr': jax.random.normal(ks[1], (D_MODEL, NUM_BANKS), dtype=jnp.float32) * s, 'br': jnp.zeros((NUM_BANKS,), dtype=jnp.float32), 'W1': jax.random.normal(ks[2], (NUM_BANKS, D_MODEL, D_HIDDEN), dtype=jnp.float32) * s, 'b1': jnp.zeros((NUM_BANKS, D_HIDDEN), dtype=jnp.float32), 'W2': jax.random.normal(ks[3], (NUM_BANKS, D_HIDDEN, D_MODEL), dtype=jnp.float32) * s, 'b2': jnp.zeros((NUM_BANKS, D_MODEL), dtype=jnp.float32)}
    _L0_ffn_in = _L0_ffn_setup()
    _d = {'L0_attn_h': _L0_attn_in['h'], 'L0_attn_Wl': _L0_attn_in['Wl'], 'L0_attn_Wr': _L0_attn_in['Wr'], 'L0_attn_att_l': _L0_attn_in['att_l'], 'L0_attn_att_r': _L0_attn_in['att_r'], 'L0_attn_Wf': _L0_attn_in['Wf'], 'L0_attn_ln_gamma': _L0_attn_in['ln_gamma'], 'L0_attn_ln_beta': _L0_attn_in['ln_beta'], 'L0_ffn_Wr': _L0_ffn_in['Wr'], 'L0_ffn_br': _L0_ffn_in['br'], 'L0_ffn_W1': _L0_ffn_in['W1'], 'L0_ffn_b1': _L0_ffn_in['b1'], 'L0_ffn_W2': _L0_ffn_in['W2'], 'L0_ffn_b2': _L0_ffn_in['b2']}
    _x0 = _d['L0_attn_h']
    _d['L0_attn_h'] = jax.random.normal(jax.random.fold_in(jax.random.key(seed), 1), (8, 256, 128), dtype=_x0.dtype)
    del _x0
    return _d

def reference(L0_attn_h, L0_attn_Wl, L0_attn_Wr, L0_attn_att_l, L0_attn_att_r, L0_attn_Wf, L0_attn_ln_gamma, L0_attn_ln_beta, L0_ffn_Wr, L0_ffn_br, L0_ffn_W1, L0_ffn_b1, L0_ffn_W2, L0_ffn_b2):

    def _L0_attn_ref(h, Wl, Wr, att_l, att_r, Wf, ln_gamma, ln_beta):
        import jax, jax.numpy as jnp
        import numpy as np
        B, N, D, H = (4, 256, 128, 8)
        HD = D // H
        TEMPER = 1.0
        LN_EPS = 1e-05

        def _leaky(x):
            return jnp.where(x > 0, x, 0.01 * x)
        b, n, d = h.shape
        fl = (h @ Wl.T).reshape(b, n, H, HD).transpose(0, 2, 1, 3)
        fr = (h @ Wr.T).reshape(b, n, H, HD).transpose(0, 2, 1, 3)
        sl = jnp.einsum('bhnd,d->bhn', _leaky(fl), att_l[0])
        sr = jnp.einsum('bhnd,d->bhn', _leaky(fr), att_r[0])
        score = (sl[:, :, :, None] + sr[:, :, None, :]) / TEMPER
        p = jax.nn.softmax(score, axis=-1)
        ctx = jnp.einsum('bhnm,bhmd->bhnd', p, fr)
        h_sa = ctx.transpose(0, 2, 1, 3).reshape(b, n, d)
        fh = h_sa @ Wf.T
        y = h + fh
        mu = jnp.mean(y, axis=-1, keepdims=True)
        var = jnp.mean(jnp.square(y - mu), axis=-1, keepdims=True)
        return (y - mu) * jax.lax.rsqrt(var + LN_EPS) * ln_gamma + ln_beta

    def _L0_ffn_ref(tensor, Wr, br, W1, b1, W2, b2):
        import jax, jax.numpy as jnp
        import numpy as np
        D_MODEL = 128
        D_HIDDEN = 512
        NUM_BANKS = 16
        NUM_SELECTED = 2
        logits = jnp.einsum('bsd,de->bse', tensor, Wr) + br
        probs = jax.nn.softmax(logits, axis=-1)
        topv, topi = jax.lax.top_k(probs, NUM_SELECTED)
        gate = jnp.sum(jax.nn.one_hot(topi, NUM_BANKS, dtype=tensor.dtype) * topv[..., None], axis=-2)
        h = jax.nn.relu(jnp.einsum('bsd,edh->bseh', tensor, W1) + b1)
        y = jnp.einsum('bseh,ehm->bsem', h, W2) + b2
        out = jnp.einsum('bse,bsem->bsm', gate, y)
        return out
    x = L0_attn_h
    x = _layernorm(x + _L0_attn_ref(x, L0_attn_Wl, L0_attn_Wr, L0_attn_att_l, L0_attn_att_r, L0_attn_Wf, L0_attn_ln_gamma, L0_attn_ln_beta), axis=-1)
    x = _layernorm(x + _L0_ffn_ref(x, L0_ffn_Wr, L0_ffn_br, L0_ffn_W1, L0_ffn_b1, L0_ffn_W2, L0_ffn_b2), axis=-1)
    return x

_drawn_inputs = setup_inputs


def setup_inputs(seed=0):
    import zlib

    import numpy as np

    out = dict(_drawn_inputs(seed))
    spreads = {'L0_attn_ln_gamma': (1.0, 0.2),
     'L0_attn_ln_beta': (0.0, 0.1),
     'L0_ffn_br': (0.0, 0.619),
     'L0_ffn_b1': (0.0, 0.8),
     'L0_ffn_b2': (0.0, 0.625)}
    factors = {'L0_attn_Wl': 8.0,
     'L0_attn_att_l': 8.0,
     'L0_ffn_Wr': 3.81,
     'L0_ffn_W1': 7.143,
     'L0_ffn_W2': 5.526}
    for name, (base, spread) in spreads.items():
        noise = np.random.default_rng([zlib.crc32(name.encode()), seed]).standard_normal(out[name].shape)
        drawn = base * np.exp(spread * noise) if base else spread * noise
        out[name] = jnp.asarray(drawn.astype(out[name].dtype))
    for name, factor in factors.items():
        out[name] = (out[name] * factor).astype(out[name].dtype)
    return out
```

```python
import numpy as np
import concourse.bass as bass
from concourse import mybir
from contextlib import ExitStack

P = 128
B, N, D = 8, 256, 128
H, HD = 8, 16
E, F = 16, 512
TOK = B * N
NT = TOK // P
NCH = 4
TC = NT // NCH
CW = TC * P
FC = F // P
K2 = 2
Q = (TOK * K2 + E * (P - 1)) // P
LN_EPS = 1e-5
YROWS = K2 * TOK + Q * P


def columns(widths):
    at, out = 0, {}
    for name, w in widths:
        out[name] = (at, at + w)
        at += w
    return out, at


PCOLS, PW = columns([("wr_t", D), ("wl_t", D), ("att_r", 1), ("att_l", 1), ("wf_t", D), ("gamma", D),
                     ("beta", D), ("gate_w", E), ("gate_b", E)])
ECOLS, EW = columns([("b1", F), ("b2", D)])
CCOLS, CWID = columns([("same_head", D), ("head_of", H), ("head_first", H), ("ident", P), ("before", P),
                       ("iota_p", P), ("pair_id", NT * K2), ("iota_e", E), ("iota_q", Q), ("pad_slot", Q),
                       ("bank_before", E * E), ("tile_floor", E * E), ("minus_half", TC), ("bank_upto", E)])


def shape_constants():
    c = np.zeros((P, CWID), np.float32)

    def put(name, a):
        lo, hi = CCOLS[name]
        c[:, lo:hi] = a

    p = np.arange(P)[:, None]
    put("same_head", p // HD == np.arange(D)[None] // HD)
    put("head_of", p // HD == np.arange(H)[None])
    put("head_first", p == HD * np.arange(H)[None])
    put("ident", p == np.arange(P)[None])
    put("before", p < np.arange(P)[None])
    put("iota_p", np.arange(P)[None])
    T, ch = np.meshgrid(np.arange(NT), np.arange(K2), indexing="ij")
    put("pair_id", TOK * ch.reshape(1, -1) + N * (T // 2).reshape(1, -1) + (T % 2).reshape(1, -1) + 2 * p + 1)
    put("iota_e", np.arange(E)[None])
    put("iota_q", np.arange(Q)[None])
    put("pad_slot", K2 * TOK + 1 + P * np.arange(Q)[None] + p)
    e = np.arange(E)
    put("bank_before", (e[None, :] < e[:, None]).reshape(1, -1))
    put("tile_floor", np.broadcast_to(P * e[None, :], (E, E)).reshape(1, -1))
    put("minus_half", -0.5)
    put("bank_upto", p <= e[None])
    return c


def routed_block(nc, h, h_t, params, bank_biases, consts, w1, w2, out, x1_rows, y_rows):
    f32, bf16, i32, u32 = mybir.dt.float32, mybir.dt.bfloat16, mybir.dt.int32, mybir.dt.uint32
    ALU, ACT, AX = mybir.AluOpType, mybir.ActivationFunctionType, mybir.AxisListType.X
    ctx = ExitStack()
    with ctx:
        def sb(name, shape, dt=f32):
            return ctx.enter_context(nc.sbuf_tensor(name, shape, dt))

        def sem(name):
            return ctx.enter_context(nc.semaphore(name))

        par = sb("par", [P, PW])
        con = sb("con", [P, CWID])
        eb = sb("eb", [E, EW])
        h_sb = sb("h_sb", [P, NT, D])
        ht_sb = sb("ht_sb", [D, TOK])
        w1_sb = sb("w1_sb", [D, E * F])
        w2_sb = sb("w2_sb", [P, E * F])

        def pv(name):
            return par[:, PCOLS[name][0]:PCOLS[name][1]]

        def cv(name):
            return con[:, CCOLS[name][0]:CCOLS[name][1]]

        ones = sb("ones", [P, P])
        ones_bf = sb("ones_bf", [P, P], bf16)
        before_bf = sb("before_bf", [P, P], bf16)
        att_r_blk = sb("att_r_blk", [D, D])
        att_l_blk = sb("att_l_blk", [D, H])
        h_beta = sb("h_beta", [P, NT, D])
        leaky_r = sb("leaky_r", [D, 2, CW])
        leaky_l = sb("leaky_l", [D, 2, CW])
        low_r = sb("low_r", [D, 2, CW])
        neg_l = sb("neg_l", [D, 2, CW])
        pos_l = sb("pos_l", [D, 2, CW])
        col = sb("col", [D, 2, CW])
        junk = sb("junk", [D, N])
        stat = sb("stat", [D, NCH, 4])
        csum = sb("csum", [D, NCH, 2])
        statd = sb("statd", [D, 2, 4, H])
        csumd = sb("csumd", [D, 2, 2, H])
        stat_tok = sb("stat_tok", [P, 2, 4, H])
        rowmax = sb("rowmax", [P, 32])
        d0 = sb("d0", [P, 32])
        d1 = sb("d1", [P, 32])
        row = sb("row", [P, 32])
        den = sb("den", [P, 32])
        rden = sb("rden", [P, 32])
        scale = sb("scale", [P, 2, TC, H])
        g_sb = sb("g_sb", [H, 2, 2, D])
        scale_t = sb("scale_t", [H, 2, CW])
        y = sb("y", [P, 2, TC, D])
        yn = sb("yn", [P, 2, TC, D])
        yg = sb("yg", [P, 2, TC, D])
        z = sb("z", [P, 2, TC, D])
        bst = sb("bst", [P, 2, TC, 6])
        mv1 = sb("mv1", [P, 2, TC, 2])
        mv2 = sb("mv2", [P, 2, TC, 2])
        mv3 = sb("mv3", [P, 2, TC, 2])
        ve = sb("ve", [P, TC])
        rstd1 = sb("rstd1", [P, 2, TC])
        rstd2 = sb("rstd2", [P, 2, TC])
        rstd3 = sb("rstd3", [P, 2, TC])
        x1 = sb("x1", [P, NT, D])
        x1t = sb("x1t", [D, 2, CW])
        lg = sb("lg", [P, NT, E])
        top = sb("top", [P, NT, 8])
        topi = sb("topi", [P, NT, 8], u32)
        pick = sb("pick", [P, NT, K2, E])
        both = sb("both", [P, NT, E], bf16)
        exin = sb("exin", [P, NT, E + 1])
        exo = sb("exo", [P, NT, E + 1])
        esum = sb("esum", [P, NT])
        g12 = sb("g12", [P, NT, K2])
        rsel = sb("rsel", [P, TC, K2, E])
        rankf = sb("rankf", [P, TC * K2])
        ranki = sb("ranki", [P, TC * K2], i32)
        rowi = sb("rowi", [P, TC * K2], i32)
        tili = sb("tili", [P, NT * K2], i32)
        rowf = sb("rowf", [P, NT * K2])
        tilf = sb("tilf", [P, NT * K2])
        place_row = sb("place_row", [P, NT * K2, P])
        ntl = sb("ntl", [P, E])
        cmp = sb("cmp", [P, E * E])
        off = sb("off", [P, E])
        osel = sb("osel", [P, NT * K2, E])
        tile_of = sb("tile_of", [P, NT * K2])
        place_tile = sb("place_tile", [P, NT * K2, Q])
        ntl_t = sb("ntl_t", [E, 1])
        end_t = sb("end_t", [E, 1])
        start_t = sb("start_t", [E, 1])
        cmp_t = sb("cmp_t", [E, E])
        bank_of_t = sb("bank_of_t", [E, Q])
        ge_start = sb("ge_start", [E, Q])
        endc = sb("endc", [1, E])
        cmp_q = sb("cmp_q", [1, Q, E])
        bankf = sb("bankf", [1, Q])
        bank = sb("bank", [1, Q + 1], i32)
        b1_tile = sb("b1_tile", [P, FC, Q])
        pad = sb("pad", [P, Q])
        padt = sb("padt", [P, Q])
        src0 = sb("src0", [P, Q], i32)
        src = sb("src", [P, Q], i32)
        dst = sb("dst", [P, Q], i32)
        gd = sb("gd", [P, NT, E])
        gd2 = sb("gd2", [P, NT, E])
        gate = sb("gate", [P, NT, E])
        gate_t = sb("gate_t", [E, 2, CW])
        base = place_row[:, 0:NT, :]
        xg, xt, yo = z[:, 0, 0:2, :], z[:, 0, 2:4, :], z[:, 1, 0:2, :]
        hid = leaky_r
        hid_t = leaky_l[:, :, :].rearrange("p k (c t) -> p k c t", c=FC)
        ya, yb, res = h_sb, ht_sb[:, :].rearrange("p (t d) -> p t d", d=D), h_beta
        t1, t2 = y, yn

        bk = [ctx.enter_context(nc.psum_tensor(f"bank{i}", [P, 512], f32)) for i in range(8)]
        ps_fr, ps_fl, ps_sr, ps_small, ps_g, ps_rt, ps_fh, ps_xt = bk
        ps_h, ps_ht, ps_x, ps_y = bk[0:2], bk[2:4], (bk[4], bk[7]), bk[5:7]
        ps_sl = ps_small[:, 0:32]
        ps_stat = ps_small[:, 32:64]
        ps_lg = ps_small[:, 64:128]
        ps_rank = ps_small[:, 128:192]

        par_in, con_in, eb_in, h_in = sem("par_in"), sem("con_in"), sem("eb_in"), sem("h_in")
        ht_in = [sem(f"ht_in{j}") for j in range(NCH)]
        w_in = sem("w_in")
        consts_ready = sem("consts_ready")
        hbeta_ready = sem("hbeta_ready")
        dve_link, act_link, pool_link = sem("dve_link"), sem("act_link"), sem("pool_link")
        low_r_ready, pos_l_ready = sem("low_r_ready"), sem("pos_l_ready")
        fr_ready, fl_ready = sem("fr_ready"), sem("fl_ready")
        leaky_r_ready, leaky_l_ready = sem("leaky_r_ready"), sem("leaky_l_ready")
        sr_ready, sl_ready = sem("sr_ready"), sem("sl_ready")
        negmax_ready, col_ready = sem("negmax_ready"), sem("col_ready")
        csumd_ready, g_ready, g_copied = sem("csumd_ready"), sem("g_ready"), sem("g_copied")
        stat_ready, d1_ready, row_ready = sem("stat_ready"), sem("d1_ready"), sem("row_ready")
        scale_ready, scale_t_ready, scale_t_copied = sem("scale_ready"), sem("scale_t_ready"), sem("scale_t_copied")
        fh_ready, y_ready, mv1_ready, rstd1_ready = sem("fh_ready"), sem("y_ready"), sem("mv1_ready"), sem("rstd1_ready")
        yn_ready, z_ready, mv2_ready, rstd2_ready = sem("yn_ready"), sem("z_ready"), sem("mv2_ready"), sem("rstd2_ready")
        x1_ready, x1t_ready, x1t_copied = sem("x1_ready"), sem("x1t_ready"), sem("x1t_copied")
        x1_out = sem("x1_out")
        lg_ready, lg_copied, both_ready, rank_ready, rank_read = (
            sem("lg_ready"), sem("lg_copied"), sem("both_ready"), sem("rank_ready"), sem("rank_read"))
        exin_ready, exo_ready, g12_ready = sem("exin_ready"), sem("exo_ready"), sem("g12_ready")
        count_ready, ntl_t_ready, end_t_ready = sem("count_ready"), sem("ntl_t_ready"), sem("end_t_ready")
        place_ready, table_ready = sem("place_ready"), sem("table_ready")
        bank_of_t_ready, b1_ready, b1_copied = sem("bank_of_t_ready"), sem("b1_ready"), sem("b1_copied")
        src_ready, dst_ready, bank_ready = sem("src_ready"), sem("dst_ready"), sem("bank_ready")
        gate_ready, gate_t_ready, gate_t_copied = sem("gate_ready"), sem("gate_t_ready"), sem("gate_t_copied")
        gb_ready, base_ready = sem("gb_ready"), sem("base_ready")
        gathered = [sem("gathered0"), sem("gathered1")]
        scattered = [sem("scattered0"), sem("scattered1")]
        xt_done, xt_copied = sem("xt_done"), sem("xt_copied")
        up_done, hid_copied = sem("up_done"), sem("hid_copied")
        hid_t_done, relu_dve, relu_act = sem("hid_t_done"), sem("relu_dve"), sem("relu_act")
        down_done, yo_ready = sem("down_done"), sem("yo_ready")
        y_in = [sem(f"y_in{j}") for j in range(NCH)]
        mv3_ready, rstd3_ready, res_ready, out_done = sem("mv3_ready"), sem("rstd3_ready"), sem("res_ready"), sem("out_done")

        block = ctx.enter_context(nc.Block())

        h_v = h.rearrange("b (p u) d -> p b (u d)", u=2)
        out_v = out.rearrange("b (p u) d -> p b (u d)", u=2)
        x1_v = x1_rows.rearrange("(b p u) d -> p b (u d)", p=P, u=2)
        ya_v = y_rows[0:TOK, :].rearrange("(b p u) d -> p b (u d)", p=P, u=2)
        yb_v = y_rows[TOK:2 * TOK, :].rearrange("(b p u) d -> p b (u d)", p=P, u=2)

        def by_batch(t, j):
            return t[:, TC * j:TC * (j + 1), :].rearrange("p (b u) d -> p b (u d)", u=2)

        @block.sync
        def _(sp):
            sp.dma_start(par[:, :], params[:, :]).then_inc(par_in, 16)
            for j in range(NCH):
                sp.dma_start(ht_sb[:, j * CW:(j + 1) * CW], h_t[:, j * CW:(j + 1) * CW]).then_inc(ht_in[j], 16)
            sp.dma_start(eb[:, :], bank_biases[:, :]).then_inc(eb_in, 16)
            for e in range(0, E, 4):
                sp.dma_start(w1_sb[:, e * F:(e + 4) * F], w1[:, e * F:(e + 4) * F]).then_inc(w_in, 16)
                sp.dma_start(w2_sb[:, e * F:(e + 4) * F], w2[:, e * F:(e + 4) * F]).then_inc(w_in, 16)
            for j in range(NCH):
                sp.wait_ge(x1_ready, j + 1)
                sp.dma_start(x1_v[:, 2 * j:2 * j + 2, :], by_batch(x1, j)).then_inc(x1_out, 16)
            sp.wait_ge(scattered[0], 16 * ((Q + 1) // 2))
            sp.wait_ge(scattered[1], 16 * (Q // 2))
            for j in range(NCH):
                sp.dma_start(by_batch(ya, j), ya_v[:, 2 * j:2 * j + 2, :]).then_inc(y_in[j], 16)
                sp.dma_start(by_batch(yb, j), yb_v[:, 2 * j:2 * j + 2, :]).then_inc(y_in[j], 16)
            for j in range(NCH):
                sp.wait_ge(res_ready, j + 1)
                sp.dma_start(out_v[:, 2 * j:2 * j + 2, :], by_batch(res, j)).then_inc(out_done, 16)
            sp.wait_ge(out_done, 16 * NCH)

        @block.scalar
        def _(act):
            act.dma_start(con[:, :], consts[:, :]).then_inc(con_in, 16)
            act.dma_start(h_sb[:, :, :].rearrange("p (b u) d -> p b (u d)", u=2), h_v).then_inc(h_in, 16)

            def attend(j):
                s = j % 2
                act.wait_ge(fr_ready, j + 1)
                nc.scalar.activation(low_r[:, s, :], ps_fr[:, :], ACT.Copy, scale=0.01).then_inc(low_r_ready, 1)
                act.wait_ge(fl_ready, j + 1)
                nc.scalar.activation(neg_l[:, s, :], ps_fl[:, :], ACT.Relu, scale=-0.01)
                nc.scalar.activation(pos_l[:, s, :], ps_fl[:, :], ACT.Relu).then_inc(pos_l_ready, 1)
                act.wait_ge(negmax_ready, j + 1)
                for b in range(2):
                    nc.scalar.activation(col[:, s, b * N:(b + 1) * N], ps_sr[:, b * N:(b + 1) * N], ACT.Exp,
                                         bias=stat[:, j, b:b + 1],
                                         accum_out=stat[:, j, 2 + b:3 + b]).then_inc(col_ready, 1)
                act.wait_ge(g_ready, j + 1)
                nc.scalar.activation(g_sb[:, s, :, :].rearrange("h b d -> h (b d)"), ps_g[0:H, 0:2 * D],
                                     ACT.Copy).then_inc(g_copied, 1)
                act.wait_ge(d1_ready, j + 1)
                nc.scalar.activation(row[:, :], d1[:, :], ACT.Exp).then_inc(row_ready, 1)
                act.wait_ge(scale_t_ready, j + 1)
                nc.scalar.activation(scale_t[:, s, :], ps_rt[0:H, :], ACT.Copy).then_inc(scale_t_copied, 1)

            def route(j):
                act.wait_ge(x1t_ready, j + 1)
                nc.scalar.activation(x1t[:, j % 2, :], ps_xt[:, :], ACT.Copy).then_inc(x1t_copied, 1)
                act.wait_ge(exin_ready, j + 1)
                nc.scalar.activation(exo[:, TC * j:TC * (j + 1), :], exin[:, TC * j:TC * (j + 1), :],
                                     ACT.Exp).then_inc(exo_ready, 1)

            attend(0)
            for j in range(NCH):
                if j + 1 < NCH:
                    attend(j + 1)
                route(j)
            act.wait_ge(b1_ready, 1)
            nc.scalar.activation(b1_tile[:, :, :].rearrange("p c q -> p (c q)"), bk[3][:, 0:FC * Q],
                                 ACT.Copy).then_inc(b1_copied, 1)
            for j in range(NCH):
                act.wait_ge(gate_t_ready, j + 1)
                nc.scalar.activation(gate_t[:, j % 2, :], bk[5][0:E, :], ACT.Copy).then_inc(gate_t_copied, 1)
            act.wait_ge(up_done, 1)
            nc.scalar.activation(hid[:, 0, :], ps_h[0][:, :], ACT.Copy).then_inc(hid_copied, 1)

            def step(q, k, last=False):
                act.wait_ge(hid_t_done, q + 1)
                for c in range(FC // 2, FC):
                    ins = nc.scalar.activation(hid_t[:, k, c, :], ps_ht[c // 2][:, (c % 2) * P:(c % 2 + 1) * P], ACT.Relu,
                                               bias=b1_tile[:, c, bass.ds(q, 1)])
                ins.then_inc(relu_act, 1)
                if not last:
                    act.wait_ge(up_done, q + 2)
                    nc.scalar.activation(hid[:, 1 - k, :], ps_h[1 - k][:, :], ACT.Copy).then_inc(hid_copied, 1)

            step(0, 0)
            step(1, 1)
            with act.Fori(2, Q - 1, 2) as q:
                step(q, 0)
                step(q + 1, 1)
            step(Q - 1, 0, last=True)

        @block.gpsimd
        def _(pool):
            links = [0]

            def link(ins):
                links[0] += 1
                ins.then_inc(pool_link, 1)
                pool.wait_ge(pool_link, links[0])

            nc.gpsimd.memset(ones[:, :], 1.0)
            nc.gpsimd.memset(ones_bf[:, :], 1.0).then_inc(consts_ready, 1)
            pool.wait_ge(h_in, 16)
            pool.wait_ge(par_in, 16)
            nc.gpsimd.tensor_tensor(h_beta[:, :, :], h_sb[:, :, :],
                                    pv("beta").unsqueeze(1).to_broadcast([P, NT, D]), ALU.add).then_inc(hbeta_ready, 1)
            pool.wait_ge(con_in, 16)
            pool.wait_ge(hbeta_ready, 1)

            def rsqrt(mv, rstd, done):
                link(nc.gpsimd.tensor_scalar(ve[:, :], mv[:, :, 1], LN_EPS, None, ALU.add))
                nc.gpsimd.tensor_tensor(rstd, ve[:, :], cv("minus_half"), ALU.pow).then_inc(done, 1)

            def leak(j):
                s = j % 2
                pool.wait_ge(pos_l_ready, j + 1)
                nc.gpsimd.tensor_tensor(leaky_l[:, s, :], pos_l[:, s, :], neg_l[:, s, :],
                                        ALU.subtract).then_inc(leaky_l_ready, 1)

            leak(0)
            for j in range(NCH):
                s = j % 2
                if j + 1 < NCH:
                    leak(j + 1)
                pool.wait_ge(mv1_ready, j + 1)
                rsqrt(mv1[:, s, :, :], rstd1[:, s, :], rstd1_ready)
                pool.wait_ge(yn_ready, j + 1)
                link(nc.gpsimd.tensor_tensor(yg[:, s, :, :], yn[:, s, :, :],
                                             pv("gamma").unsqueeze(1).to_broadcast([P, TC, D]), ALU.mult))
                nc.gpsimd.tensor_tensor(z[:, s, :, :], yg[:, s, :, :], h_beta[:, TC * j:TC * (j + 1), :],
                                        ALU.add).then_inc(z_ready, 1)
                pool.wait_ge(mv2_ready, j + 1)
                rsqrt(mv2[:, s, :, :], rstd2[:, s, :], rstd2_ready)
            pool.wait_ge(g12_ready, NCH)
            nc.gpsimd.tensor_tensor(gd[:, :, :], pick[:, :, 0, :],
                                    g12[:, :, 0:1].to_broadcast([P, NT, E]), ALU.mult)
            link(nc.gpsimd.tensor_tensor(gd2[:, :, :], pick[:, :, 1, :],
                                         g12[:, :, 1:2].to_broadcast([P, NT, E]), ALU.mult))
            nc.gpsimd.tensor_tensor(gate[:, :, :], gd[:, :, :], gd2[:, :, :], ALU.add).then_inc(gate_ready, 1)

            def fetch(q):
                if q >= 2:
                    pool.wait_ge(xt_done, q - 1)
                nc.gpsimd.indirect_dma_start(xg[:, q % 2, :], None, x1_rows[:, :],
                                             bass.IndirectOffsetOnAxis(ap=src[:, q:q + 1], axis=0)
                                             ).then_inc(gathered[q % 2], 16)

            def put(q):
                pool.wait_ge(yo_ready, q + 1)
                nc.gpsimd.indirect_dma_start(y_rows[:, :], bass.IndirectOffsetOnAxis(ap=dst[:, q:q + 1], axis=0),
                                             yo[:, q % 2, :], None).then_inc(scattered[q % 2], 16)

            pool.wait_ge(x1_out, 16 * NCH)
            pool.wait_ge(src_ready, 1)
            for q in range(4):
                fetch(q)
            pool.wait_ge(dst_ready, 1)
            for q in range(Q):
                if q + 4 < Q:
                    fetch(q + 4)
                put(q)

            for j in range(NCH):
                pool.wait_ge(mv3_ready, j + 1)
                rsqrt(mv3[:, j % 2, :, :], rstd3[:, j % 2, :], rstd3_ready)

        @block.vector
        def _(dve):
            links = [0]

            def link(ins):
                links[0] += 1
                ins.then_inc(dve_link, 1)
                dve.wait_ge(dve_link, links[0])

            dve.wait_ge(par_in, 16)
            dve.wait_ge(con_in, 16)
            nc.vector.tensor_scalar(att_r_blk[:, :], cv("same_head"), pv("att_r"), None, ALU.mult)
            nc.vector.tensor_scalar(att_l_blk[:, :], cv("head_of"), pv("att_l"), None, ALU.mult)
            nc.vector.tensor_copy(before_bf[:, :], cv("before")).then_inc(consts_ready, 1)

            def attend(j):
                s = j % 2
                dve.wait_ge(low_r_ready, j + 1)
                nc.vector.tensor_tensor(leaky_r[:, s, :], ps_fr[:, :], low_r[:, s, :], ALU.max).then_inc(leaky_r_ready, 1)
                dve.wait_ge(sr_ready, j + 1)
                nc.vector.tensor_reduce(stat[:, j, 0:2], ps_sr[:, :].rearrange("p (b n) -> p b n", b=2), AX,
                                        ALU.max, negate=True).then_inc(negmax_ready, 1)
                for b in range(2):
                    dve.wait_ge(col_ready, 2 * j + b + 1)
                    link(nc.vector.scalar_tensor_tensor(junk[:, :], col[:, s, b * N:(b + 1) * N], 1.0,
                                                        ps_fr[:, b * N:(b + 1) * N], ALU.mult, ALU.mult,
                                                        accum_out=csum[:, j, b:b + 1]))
                nc.vector.tensor_tensor(csumd[:, s, :, :], cv("head_of").unsqueeze(1).to_broadcast([D, 2, H]),
                                        csum[:, j, :].unsqueeze(2).to_broadcast([D, 2, H]), ALU.mult)
                nc.vector.tensor_tensor(statd[:, s, :, :], cv("head_first").unsqueeze(1).to_broadcast([D, 4, H]),
                                        stat[:, j, :].unsqueeze(2).to_broadcast([D, 4, H]),
                                        ALU.mult).then_inc(csumd_ready, 1)
                dve.wait_ge(stat_ready, j + 1)
                dve.wait_ge(sl_ready, j + 1)
                link(nc.vector.tensor_copy(stat_tok[:, s, :, :].rearrange("p k h -> p (k h)"), ps_stat))

                def per_tile(a):
                    return a.unsqueeze(2).to_broadcast([P, 2, 2, H])

                def quad(a):
                    return a.rearrange("p (b u h) -> p b u h", b=2, u=2)

                negr, tot = per_tile(stat_tok[:, s, 0:2, :]), per_tile(stat_tok[:, s, 2:4, :])
                link(nc.vector.tensor_tensor(quad(rowmax[:, :]), quad(ps_sl), negr, ALU.subtract))
                link(nc.vector.tensor_tensor(d0[:, :], ps_sl, rowmax[:, :], ALU.subtract))
                nc.vector.tensor_tensor(quad(d1[:, :]), quad(d0[:, :]), negr, ALU.subtract).then_inc(d1_ready, 1)
                dve.wait_ge(row_ready, j + 1)
                link(nc.vector.tensor_tensor(quad(den[:, :]), quad(row[:, :]), tot, ALU.mult))
                link(nc.vector.reciprocal(rden[:, :], den[:, :]))
                nc.vector.tensor_tensor(scale[:, s, :, :].rearrange("p t h -> p (t h)"), row[:, :], rden[:, :],
                                        ALU.mult).then_inc(scale_ready, 1)

            def moments(x, mv, done):
                for t in range(TC):
                    ins = nc.vector.bn_stats(bst[:, 0, t, :], x[:, t, :])
                link(ins)
                for t in range(TC):
                    ins = nc.vector.bn_aggr(mv[:, t, :], bst[:, 0, t, :])
                ins.then_inc(done, 1)

            def normalise(dst_, x, mv, rstd, done):
                for t in range(TC):
                    ins = nc.vector.tensor_scalar(dst_[:, t, :], x[:, t, :], mv[:, t, 0:1], rstd[:, t:t + 1],
                                                  ALU.subtract, ALU.mult)
                ins.then_inc(done, 1)

            def norms(j):
                s = j % 2
                T = slice(TC * j, TC * (j + 1))
                if j == 0:
                    dve.wait_ge(h_in, 16)
                dve.wait_ge(fh_ready, j + 1)
                link(nc.vector.tensor_tensor(y[:, s, :, :].rearrange("p t d -> p (t d)"), ps_fh[:, :],
                                             h_sb[:, T, :].rearrange("p t d -> p (t d)"), ALU.add))
                moments(y[:, s, :, :], mv1[:, s, :, :], mv1_ready)
                dve.wait_ge(rstd1_ready, j + 1)
                normalise(yn[:, s, :, :], y[:, s, :, :], mv1[:, s, :, :], rstd1[:, s, :], yn_ready)
                dve.wait_ge(z_ready, j + 1)
                moments(z[:, s, :, :], mv2[:, s, :, :], mv2_ready)
                dve.wait_ge(rstd2_ready, j + 1)
                normalise(x1[:, T, :], z[:, s, :, :], mv2[:, s, :, :], rstd2[:, s, :], x1_ready)

            def route(j):
                T = slice(TC * j, TC * (j + 1))
                T2 = slice(TC * K2 * j, TC * K2 * (j + 1))
                dve.wait_ge(lg_ready, j + 1)
                link(nc.vector.tensor_tensor(lg[:, T, :], ps_lg.rearrange("p (t e) -> p t e", t=TC),
                                             pv("gate_b").unsqueeze(1).to_broadcast([P, TC, E]), ALU.add))
                for t in range(TC * j, TC * (j + 1)):
                    ins = nc.vector.max(top[:, t, :], lg[:, t, :])
                link(ins)
                for t in range(TC * j, TC * (j + 1)):
                    ins = nc.vector.max_index(topi[:, t, :], top[:, t, :], lg[:, t, :])
                link(ins)
                link(nc.vector.tensor_tensor(
                    pick[:, T, :, :], cv("iota_e").unsqueeze(1).unsqueeze(1).to_broadcast([P, TC, K2, E]),
                    topi[:, T, 0:K2].unsqueeze(3).to_broadcast([P, TC, K2, E]), ALU.is_equal))
                nc.vector.tensor_tensor(both[:, T, :], pick[:, T, 0, :], pick[:, T, 1, :],
                                        ALU.add).then_inc(both_ready, 1)
                nc.vector.tensor_tensor(exin[:, T, 0:E], lg[:, T, :], top[:, T, 0:1].to_broadcast([P, TC, E]),
                                        ALU.subtract)
                nc.vector.tensor_tensor(exin[:, T, E:E + 1], top[:, T, 1:2], top[:, T, 0:1],
                                        ALU.subtract).then_inc(exin_ready, 1)
                dve.wait_ge(rank_ready, j + 1)
                nc.vector.tensor_tensor(
                    rsel[:, :, :, :], pick[:, T, :, :],
                    ps_rank.rearrange("p (t e) -> p t e", t=TC).unsqueeze(2).to_broadcast([P, TC, K2, E]), ALU.mult
                ).then_inc(rank_read, 1)
                dve.wait_ge(rank_read, j + 1)
                link(nc.vector.tensor_reduce(rankf[:, :], rsel[:, :, :, :].rearrange("p t k e -> p (t k) e"), AX,
                                             ALU.add))
                link(nc.vector.tensor_copy(ranki[:, :], rankf[:, :]))
                nc.vector.tensor_single_scalar(tili[:, T2], ranki[:, :], 7, ALU.arith_shift_right)
                link(nc.vector.tensor_single_scalar(rowi[:, :], ranki[:, :], P - 1, ALU.bitwise_and))
                nc.vector.tensor_copy(tilf[:, T2], tili[:, T2])
                link(nc.vector.tensor_copy(rowf[:, T2], rowi[:, :]))
                for k in range(TC * K2 * j, TC * K2 * (j + 1)):
                    nc.vector.tensor_scalar(place_row[:, k, :], cv("iota_p"), rowf[:, k:k + 1],
                                            cv("pair_id")[:, k:k + 1], ALU.is_equal, ALU.mult)
                dve.wait_ge(exo_ready, j + 1)
                link(nc.vector.tensor_reduce(esum[:, T], exo[:, T, 0:E], AX, ALU.add))
                link(nc.vector.reciprocal(g12[:, T, 0], esum[:, T]))
                nc.vector.tensor_tensor(g12[:, T, 1], exo[:, T, E], g12[:, T, 0], ALU.mult).then_inc(g12_ready, 1)

            attend(0)
            for j in range(NCH):
                if j + 1 < NCH:
                    attend(j + 1)
                norms(j)
                route(j)

            dve.wait_ge(count_ready, 1)
            cnt = bk[4][:, 0:E]
            link(nc.vector.tensor_tensor(cmp[:, :].rearrange("p (e k) -> p e k", e=E),
                                         cv("tile_floor").rearrange("p (e k) -> p e k", e=E),
                                         cnt.unsqueeze(2).to_broadcast([P, E, E]), ALU.is_lt))
            link(nc.vector.tensor_reduce(ntl[:, :], cmp[:, :].rearrange("p (e k) -> p e k", e=E), AX, ALU.add))
            link(nc.vector.tensor_tensor(cmp[:, :].rearrange("p (e k) -> p e k", e=E),
                                         cv("bank_before").rearrange("p (e k) -> p e k", e=E),
                                         ntl[:, :].unsqueeze(1).to_broadcast([P, E, E]), ALU.mult))
            link(nc.vector.tensor_reduce(off[:, :], cmp[:, :].rearrange("p (e k) -> p e k", e=E), AX, ALU.add))
            link(nc.vector.tensor_tensor(osel[:, :, :], pick[:, :, :, :].rearrange("p t k e -> p (t k) e"),
                                         off[:, :].unsqueeze(1).to_broadcast([P, NT * K2, E]), ALU.mult))
            link(nc.vector.tensor_reduce(tile_of[:, :], osel[:, :, :], AX, ALU.add))
            link(nc.vector.tensor_tensor(tile_of[:, :], tile_of[:, :], tilf[:, :], ALU.add))
            for g in range(4):
                k = slice(8 * g, 8 * (g + 1))
                nc.vector.tensor_tensor(place_tile[:, k, :], cv("iota_q").unsqueeze(1).to_broadcast([P, 8, Q]),
                                        tile_of[:, k].unsqueeze(2).to_broadcast([P, 8, Q]),
                                        ALU.is_equal).then_inc(place_ready, 1)
            nc.vector.tensor_scalar(cmp_t[:, :], con[0:E, CCOLS["tile_floor"][0]:CCOLS["tile_floor"][0] + E],
                                    bk[4][0:E, 64:65], None, ALU.is_lt)
            link(nc.vector.tensor_single_scalar(endc[:, :], off[0:1, :], 0.0, ALU.add))
            nc.vector.tensor_reduce(ntl_t[:, :], cmp_t[:, :], AX, ALU.add).then_inc(ntl_t_ready, 1)
            link(nc.vector.tensor_tensor(endc[:, :], off[0:1, :], ntl[0:1, :], ALU.add))
            link(nc.vector.tensor_tensor(cmp_q[:, :, :],
                                         endc[:, :].unsqueeze(1).to_broadcast([1, Q, E]),
                                         con[0:1, CCOLS["iota_q"][0]:CCOLS["iota_q"][1]].unsqueeze(2)
                                         .to_broadcast([1, Q, E]), ALU.is_le))
            link(nc.vector.tensor_reduce(bankf[:, :], cmp_q[:, :, :], AX, ALU.add))
            nc.vector.tensor_scalar(bank[:, 0:Q], bankf[:, :], float(E - 1), None, ALU.min).then_inc(bank_ready, 1)
            dve.wait_ge(end_t_ready, 1)
            iq = con[0:E, CCOLS["iota_q"][0]:CCOLS["iota_q"][1]]
            link(nc.vector.tensor_copy(end_t[:, :], bk[4][0:E, 65:66]))
            link(nc.vector.tensor_tensor(start_t[:, :], end_t[:, :], ntl_t[:, :], ALU.subtract))
            link(nc.vector.tensor_scalar(ge_start[:, :], iq, start_t[:, 0:1], None, ALU.is_ge))
            nc.vector.scalar_tensor_tensor(bank_of_t[:, :], iq, end_t[:, 0:1], ge_start[:, :], ALU.is_lt,
                                           ALU.mult).then_inc(bank_of_t_ready, 1)
            dve.wait_ge(table_ready, 1)
            tab = bk[6][:, 0:Q]
            link(nc.vector.tensor_scalar(src0[:, :], tab, -1.0, 0.0, ALU.add, ALU.max))
            nc.vector.tensor_single_scalar(src[:, :], src0[:, :], TOK - 1, ALU.bitwise_and).then_inc(src_ready, 1)
            link(nc.vector.tensor_scalar(pad[:, :], tab, 0.0, None, ALU.is_equal))
            link(nc.vector.tensor_tensor(padt[:, :], pad[:, :], cv("pad_slot"), ALU.mult))
            nc.vector.scalar_tensor_tensor(dst[:, :], tab, -1.0, padt[:, :], ALU.add, ALU.add).then_inc(dst_ready, 1)

            for j in range(NCH):
                T = slice(TC * j, TC * (j + 1))
                dve.wait_ge(gb_ready, j + 1)
                nc.vector.tensor_tensor(base[:, T, :].rearrange("p t d -> p (t d)"), bk[7][:, :],
                                        x1[:, T, :].rearrange("p t d -> p (t d)"), ALU.add).then_inc(base_ready, 1)

            def copy_xt(q, k):
                dve.wait_ge(xt_done, q + 1)
                nc.vector.tensor_copy(xt[:, k, :], ps_x[k][:, 0:P]).then_inc(xt_copied, 1)

            def copy_y(q, k, before):
                dve.wait_ge(down_done, q + 1)
                if before is not None:
                    dve.wait_ge(scattered[k], 16 * before)
                nc.vector.tensor_copy(yo[:, k, :], ps_y[k][:, 0:D]).then_inc(yo_ready, 1)

            def relu_half(q, k):
                dve.wait_ge(hid_t_done, q + 1)
                for c in range(FC // 2):
                    ins = nc.vector.tensor_scalar(hid_t[:, k, c, :], ps_ht[c // 2][:, (c % 2) * P:(c % 2 + 1) * P],
                                                  b1_tile[:, c, bass.ds(q, 1)], 0.0, ALU.add, ALU.max)
                ins.then_inc(relu_dve, 1)

            dve.wait_ge(b1_copied, 1)
            copy_xt(0, 0)
            copy_xt(1, 1)
            copy_xt(2, 0)
            relu_half(0, 0)
            copy_y(0, 0, None)
            copy_xt(3, 1)
            relu_half(1, 1)
            copy_y(1, 1, None)
            copy_xt(4, 0)
            relu_half(2, 0)
            with dve.Fori(1, (Q - 3) // 2) as i:
                copy_y(2 * i, 0, i)
                copy_xt(2 * i + 3, 1)
                relu_half(2 * i + 1, 1)
                copy_y(2 * i + 1, 1, i)
                copy_xt(2 * i + 4, 0)
                relu_half(2 * i + 2, 0)
            for q in range(Q - 2, Q):
                copy_y(q - 1, (q - 1) % 2, (q - 1) // 2)
                if q + 2 < Q:
                    copy_xt(q + 2, q % 2)
                relu_half(q, q % 2)
            copy_y(Q - 1, 0, (Q - 1) // 2)

            for j in range(NCH):
                s = j % 2
                dve.wait_ge(y_in[j], 32)
                for t in range(TC):
                    ins = nc.vector.scalar_tensor_tensor(t1[:, s, t, :], ya[:, TC * j + t, :],
                                                         g12[:, TC * j + t, 0:1], base[:, TC * j + t, :],
                                                         ALU.mult, ALU.add)
                link(ins)
                for t in range(TC):
                    ins = nc.vector.scalar_tensor_tensor(t2[:, s, t, :], yb[:, TC * j + t, :],
                                                         g12[:, TC * j + t, 1:2], t1[:, s, t, :],
                                                         ALU.mult, ALU.add)
                link(ins)
                moments(t2[:, s, :, :], mv3[:, s, :, :], mv3_ready)
                dve.wait_ge(rstd3_ready, j + 1)
                normalise(res[:, TC * j:TC * (j + 1), :], t2[:, s, :, :], mv3[:, s, :, :], rstd3[:, s, :], res_ready)

        @block.tensor
        def _(pe):
            pe.wait_ge(par_in, 16)
            pe.wait_ge(con_in, 16)
            pe.wait_ge(consts_ready, 2)
            ident = cv("ident")

            def attend(j):
                s = j % 2
                pe.wait_ge(ht_in[j], 16)
                rows = ht_sb[:, j * CW:(j + 1) * CW]
                if j:
                    pe.wait_ge(csumd_ready, j)
                nc.tensor.matmul(ps_fr[:, :], pv("wr_t"), rows, start=True, stop=True).then_inc(fr_ready, 1)
                nc.tensor.matmul(ps_fl[:, :], pv("wl_t"), rows, start=True, stop=True).then_inc(fl_ready, 1)
                pe.wait_ge(leaky_r_ready, j + 1)
                nc.tensor.matmul(ps_sr[:, :], att_r_blk[:, :], leaky_r[:, s, :], start=True,
                                 stop=True).then_inc(sr_ready, 1)
                pe.wait_ge(leaky_l_ready, j + 1)
                if j:
                    pe.wait_ge(scale_ready, j)
                if j >= 2:
                    pe.wait_ge(rank_read, j - 1)
                for t in range(TC):
                    ins = nc.tensor.matmul(ps_sl[:, H * t:H * (t + 1)], leaky_l[:, s, t * P:(t + 1) * P],
                                           att_l_blk[:, :], start=True, stop=True)
                ins.then_inc(sl_ready, 1)
                pe.wait_ge(csumd_ready, j + 1)
                nc.tensor.matmul(ps_stat, ones[:, :], statd[:, s, :, :].rearrange("p k h -> p (k h)"), start=True,
                                 stop=True).then_inc(stat_ready, 1)
                if j:
                    pe.wait_ge(g_copied, j)
                for b in range(2):
                    ins = nc.tensor.matmul(ps_g[0:H, b * D:(b + 1) * D], csumd[:, s, b, :], pv("wf_t"), start=True,
                                           stop=True)
                ins.then_inc(g_ready, 1)
                pe.wait_ge(scale_ready, j + 1)
                if j:
                    pe.wait_ge(scale_t_copied, j)
                for t in range(TC):
                    ins = nc.tensor.transpose(ps_rt[0:H, t * P:(t + 1) * P], scale[:, s, t, :], ident)
                ins.then_inc(scale_t_ready, 1)

            def project(j):
                s = j % 2
                pe.wait_ge(g_copied, j + 1)
                pe.wait_ge(scale_t_copied, j + 1)
                if j:
                    pe.wait_ge(mv1_ready, j)
                for t in range(TC):
                    ins = nc.tensor.matmul(ps_fh[:, t * P:(t + 1) * P], scale_t[:, s, t * P:(t + 1) * P],
                                           g_sb[:, s, t // 2, :], start=True, stop=True)
                ins.then_inc(fh_ready, 1)

            def route(j):
                s = j % 2
                pe.wait_ge(x1_ready, j + 1)
                if j:
                    pe.wait_ge(x1t_copied, j)
                for t in range(TC):
                    ins = nc.tensor.transpose(ps_xt[:, t * P:(t + 1) * P], x1[:, TC * j + t, :], ident)
                ins.then_inc(x1t_ready, 1)
                pe.wait_ge(x1t_copied, j + 1)
                for t in range(TC):
                    ins = nc.tensor.matmul(ps_lg[:, E * t:E * (t + 1)], x1t[:, s, t * P:(t + 1) * P],
                                           pv("gate_w"), start=True, stop=True)
                ins.then_inc(lg_ready, 1)
                pe.wait_ge(both_ready, j + 1)
                first = True
                for t in range(TC * (j + 1)):
                    lo = max(t - TC * j + 1, 0)
                    if lo < TC:
                        nc.tensor.matmul(ps_rank[:, E * lo:E * TC], ones_bf[:, :],
                                         both[:, t, :].unsqueeze(1).to_broadcast([P, TC - lo, E]),
                                         start=first, stop=False, skip_group_check=True)
                        first = False
                for t in range(TC):
                    ins = nc.tensor.matmul(ps_rank[:, E * t:E * (t + 1)], before_bf[:, :], both[:, TC * j + t, :],
                                           start=False, stop=t == TC - 1, skip_group_check=True)
                ins.then_inc(rank_ready, 1)

            attend(0)
            for j in range(NCH):
                if j + 1 < NCH:
                    attend(j + 1)
                project(j)
                route(j)

            for t in range(NT):
                nc.tensor.matmul(bk[4][:, 0:E], ones_bf[:, :], both[:, t, :], start=t == 0, stop=t == NT - 1)
            for t in range(NT):
                ins = nc.tensor.matmul(bk[4][0:E, 64:65], both[:, t, :], ones_bf[:, 0:1], start=t == 0,
                                       stop=t == NT - 1)
            ins.then_inc(count_ready, 1)
            for k in range(NT * K2):
                if k % 8 == 0:
                    pe.wait_ge(place_ready, k // 8 + 1)
                ins = nc.tensor.matmul(bk[6][:, 0:Q], place_row[:, k, :], place_tile[:, k, :], start=k == 0,
                                       stop=k == NT * K2 - 1)
            ins.then_inc(table_ready, 1)
            pe.wait_ge(ntl_t_ready, 1)
            nc.tensor.matmul(bk[4][0:E, 65:66], con[0:E, CCOLS["bank_upto"][0]:CCOLS["bank_upto"][1]],
                             ntl_t[:, :], start=True, stop=True).then_inc(end_t_ready, 1)
            pe.wait_ge(bank_of_t_ready, 1)
            pe.wait_ge(eb_in, 16)
            for c in range(FC):
                ins = nc.tensor.matmul(bk[3][:, c * Q:(c + 1) * Q], eb[:, c * P:(c + 1) * P], bank_of_t[:, :],
                                       start=True, stop=True)
            ins.then_inc(b1_ready, 1)
            pe.wait_ge(gate_ready, 1)
            for j in range(NCH):
                if j:
                    pe.wait_ge(gate_t_copied, j)
                for t in range(TC):
                    ins = nc.tensor.transpose(bk[5][0:E, t * P:(t + 1) * P], gate[:, TC * j + t, :], ident)
                ins.then_inc(gate_t_ready, 1)
                pe.wait_ge(gate_t_copied, j + 1)
                if j:
                    pe.wait_ge(base_ready, j)
                for t in range(TC):
                    ins = nc.tensor.matmul(bk[7][:, t * P:(t + 1) * P], gate_t[:, j % 2, t * P:(t + 1) * P],
                                           eb[:, F:F + D], start=True, stop=True)
                ins.then_inc(gb_ready, 1)

            def turn_x(q, k, count):
                pe.wait_ge(gathered[k], 16 * count)
                if not isinstance(q, int) or q >= 2:
                    pe.wait_ge(xt_copied, q - 1)
                nc.tensor.transpose(ps_x[k][:, 0:P], xg[:, k, :], ident).then_inc(xt_done, 1)

            def bank_at(q):
                return pe.value_load(bank[0:1, bass.ds(q, 1)], min_val=0, max_val=E - 1)

            def up(q, k):
                pe.wait_ge(xt_copied, q + 1)
                nc.tensor.matmul(ps_h[k][:, :], xt[:, k, :], w1_sb[:, bass.ds(bank_at(q) * F, F)], start=True,
                                 stop=True).then_inc(up_done, 1)

            def turn_hidden(q, k):
                pe.wait_ge(hid_copied, q + 1)
                for c in range(FC):
                    ins = nc.tensor.transpose(ps_ht[c // 2][:, (c % 2) * P:(c % 2 + 1) * P], hid[:, k, c * P:(c + 1) * P], ident)
                ins.then_inc(hid_t_done, 1)

            def down(q, k):
                e = bank_at(q)
                pe.wait_ge(relu_dve, q + 1)
                pe.wait_ge(relu_act, q + 1)
                if not isinstance(q, int) or q >= 2:
                    pe.wait_ge(yo_ready, q - 1)
                for c in range(FC):
                    ins = nc.tensor.matmul(ps_y[k][:, 0:D], hid_t[:, k, c, :],
                                           w2_sb[:, bass.ds(e * F + c * P, P)], start=c == 0, stop=c == FC - 1)
                ins.then_inc(down_done, 1)

            pe.wait_ge(bank_ready, 1)
            pe.wait_ge(b1_copied, 1)
            pe.wait_ge(base_ready, NCH)
            pe.wait_ge(w_in, 16 * E // 2)
            turn_x(0, 0, 1)
            up(0, 0)
            turn_x(1, 1, 1)

            def step(q, k, count):
                if count is not None:
                    turn_x(q + 2, k, count)
                turn_hidden(q, k)
                if not isinstance(q, int) or q + 1 < Q:
                    up(q + 1, 1 - k)
                down(q, k)

            step(0, 0, 2)
            step(1, 1, 2)
            with pe.Fori(1, (Q - 3) // 2) as i:
                step(2 * i, 0, i + 2)
                step(2 * i + 1, 1, i + 2)
            for q in range(Q - 3, Q):
                step(q, q % 2, (q + 2) // 2 + 1 if q + 2 < Q else None)


def kernel(L0_attn_h, L0_attn_Wl, L0_attn_Wr, L0_attn_att_l, L0_attn_att_r, L0_attn_Wf, L0_attn_ln_gamma,
           L0_attn_ln_beta, L0_ffn_Wr, L0_ffn_br, L0_ffn_W1, L0_ffn_b1, L0_ffn_W2, L0_ffn_b2):
    import concourse.bacc as bacc
    from concourse.bass_utils import run_bass_kernel_spmd

    a = [np.asarray(x) for x in (L0_attn_h, L0_attn_Wl, L0_attn_Wr, L0_attn_att_l, L0_attn_att_r, L0_attn_Wf,
                                 L0_attn_ln_gamma, L0_attn_ln_beta, L0_ffn_Wr, L0_ffn_br, L0_ffn_W1, L0_ffn_b1,
                                 L0_ffn_W2, L0_ffn_b2)]
    h, wl, wr, att_l, att_r, wf, gamma, beta, gw, gb, w1, b1, w2, b2 = a

    def rows(v):
        return np.broadcast_to(v.reshape(1, -1), (P, v.size))

    params = np.concatenate([wr.T, wl.T, np.tile(att_r.reshape(-1), H)[:, None], np.tile(att_l.reshape(-1), H)[:, None],
                             wf.T, rows(gamma), rows(beta), gw, rows(gb)], axis=1)
    ins = {
        "h": h,
        "h_t": h.reshape(B, P, 2, D).transpose(3, 0, 2, 1).reshape(D, TOK),
        "params": params,
        "bank_biases": np.concatenate([b1, b2], axis=1),
        "consts": shape_constants(),
        "w1": w1.transpose(1, 0, 2).reshape(D, E * F),
        "w2": w2.reshape(E, FC, P, D).transpose(2, 0, 1, 3).reshape(P, E * F),
    }
    ins = {k: np.ascontiguousarray(v) for k, v in ins.items()}
    nc = bacc.Bacc("TRN2", target_bir_lowering=False, num_devices=1)
    aps = [nc.dram_tensor(k, v.shape, mybir.dt.from_np(v.dtype), kind="ExternalInput").ap() for k, v in ins.items()]
    out = nc.dram_tensor("out", (B, N, D), mybir.dt.float32, kind="ExternalOutput").ap()
    x1_rows = nc.dram_tensor("x1_rows", (TOK, D), mybir.dt.float32, kind="Internal").ap()
    y_rows = nc.dram_tensor("y_rows", (YROWS, D), mybir.dt.float32, kind="Internal").ap()
    routed_block(nc, *aps, out, x1_rows, y_rows)
    r = run_bass_kernel_spmd(nc, [ins], core_ids=[0])
    return r.results[0]["out"]
```

```python
import numpy as np
import concourse.bass as bass
from concourse import mybir
from contextlib import ExitStack

P = 128
B, N, D = 8, 256, 128
H, HD = 8, 16
E, F = 16, 512
TOK = B * N
NT = TOK // P
NCH = 4
TC = NT // NCH
CW = TC * P
FC = F // P
K2 = 2
Q = (TOK * K2 + E * (P - 1)) // P
LN_EPS = 1e-5
REGION = TOK + P
REG_T = REGION // P
XROWS = E * REGION + P
W = D + 3
DEPTH = 4
YROWS = K2 * TOK + Q * P


def columns(widths):
    at, out = 0, {}
    for name, w in widths:
        out[name] = (at, at + w)
        at += w
    return out, at


PCOLS0, PW0 = columns([("wr_t", D), ("wl_t", D), ("att_r", 1), ("att_l", 1)])
PCOLS, PW = columns([("wf_t", D), ("gamma", D), ("beta", D), ("gate_w", E), ("gate_b", E), ("b1_t", E * FC)])
CCOLS0, CWID0 = columns([("same_head", D), ("head_of", H), ("head_first", H)])
CCOLS, CWID = columns([("ident", P), ("before", P), ("token", NT), ("iota_e", E), ("dump", Q), ("pad_row", 3),
                       ("region", E), ("bank_before", E * E), ("tile_floor", E * E), ("tile", 1), ("start", E),
                       ("minus_half", TC)])


def shape_constants():
    c0, c = np.zeros((P, CWID0), np.float32), np.zeros((P, CWID), np.float32)

    def put(name, a):
        where, (lo, hi) = (c0, CCOLS0[name]) if name in CCOLS0 else (c, CCOLS[name])
        where[:, lo:hi] = a

    p = np.arange(P)[:, None]
    e = np.arange(E)
    put("same_head", p // HD == np.arange(D)[None] // HD)
    put("head_of", p // HD == np.arange(H)[None])
    put("head_first", p == HD * np.arange(H)[None])
    put("ident", p == np.arange(P)[None])
    put("before", p < np.arange(P)[None])
    put("token", N * (np.arange(NT)[None] // 2) + 2 * p + np.arange(NT)[None] % 2)
    put("iota_e", e[None])
    put("dump", P * np.arange(Q)[None])
    put("pad_row", np.concatenate([K2 * TOK + p, np.full_like(p, -1), np.ones_like(p)], axis=1))
    put("region", REGION * e[None])
    put("bank_before", (e[None, :] < e[:, None]).reshape(1, -1))
    put("tile_floor", np.broadcast_to(P * e[None, :], (E, E)).reshape(1, -1))
    put("tile", p)
    put("start", REG_T * e[None] + p - E * REG_T)
    put("minus_half", -0.5)
    return c0, c


def routed_block(nc, h, h_t, first_params, params, first_consts, consts, w1, w2, b2, out, x_rows, y_rows):
    f32, bf16, f16 = mybir.dt.float32, mybir.dt.bfloat16, mybir.dt.float16
    i32, u32 = mybir.dt.int32, mybir.dt.uint32
    ALU, ACT, AX = mybir.AluOpType, mybir.ActivationFunctionType, mybir.AxisListType.X
    ctx = ExitStack()
    with ctx:
        def sb(name, shape, dt=f32):
            return ctx.enter_context(nc.sbuf_tensor(name, shape, dt))

        def sem(name):
            return ctx.enter_context(nc.semaphore(name))

        par0, par, con0, con = sb("par0", [P, PW0]), sb("par", [P, PW]), sb("con0", [P, CWID0]), sb("con", [P, CWID])
        views = {}
        for t, cols in ((par0, PCOLS0), (par, PCOLS), (con0, CCOLS0), (con, CCOLS)):
            for name, (lo, hi) in cols.items():
                views[name] = t[:, lo:hi]
        h_sb = sb("h_sb", [P, NT, D])
        ht_sb = sb("ht_sb", [D, TOK])
        w1_sb = sb("w1_sb", [D, E * F])
        w2_sb = sb("w2_sb", [P, E * F])
        b2_sb = sb("b2_sb", [P, E * D])

        ones = sb("ones", [P, P])
        ones_bf = sb("ones_bf", [P, P], bf16)
        before_bf = sb("before_bf", [P, P], bf16)
        att_r_blk = sb("att_r_blk", [D, D])
        att_l_blk = sb("att_l_blk", [D, H])
        h_beta = sb("h_beta", [P, NT, D])
        leaky_r = sb("leaky_r", [D, 2, CW])
        leaky_l = sb("leaky_l", [D, 2, CW])
        neg_l = sb("neg_l", [D, 2, CW])
        col = sb("col", [D, 2, CW])
        junk = sb("junk", [D, 2, N])
        stat = sb("stat", [D, NCH, 4])
        csum = sb("csum", [D, NCH, 2])
        statd = sb("statd", [D, 2, 4, H])
        csumd = sb("csumd", [D, 2, 2, H])
        stat_tok = sb("stat_tok", [P, 2, 4, H])
        rowmax = sb("rowmax", [P, 32])
        d0 = sb("d0", [P, 32])
        d1 = sb("d1", [P, 32])
        row = sb("row", [P, 32])
        den = sb("den", [P, 32])
        rden = sb("rden", [P, 32])
        scale = sb("scale", [P, 2, TC, H])
        g_sb = sb("g_sb", [H, 2, 2, D])
        scale_t = sb("scale_t", [H, 2, CW])
        bst = sb("bst", [P, TC, 6])
        mv = sb("mv", [P, 3, NCH, TC, 2])
        ve = sb("ve", [P, 3, NCH, TC])
        rstd = sb("rstd", [P, 3, NCH, TC])
        shift = sb("shift", [P, 3, NCH, TC])
        x1_rows = sb("x1_rows", [P, NT, W])
        x1t = sb("x1t", [D, 2, CW])
        lg = sb("lg", [P, NT, E])
        top = sb("top", [P, NT, 8])
        topi = sb("topi", [P, NT, 8], u32)
        pick = sb("pick", [P, NT, K2, E])
        both = sb("both", [P, NT, E], bf16)
        exin = sb("exin", [P, NT, E + 1])
        exo = sb("exo", [P, NT, E + 1])
        esum = sb("esum", [P, NT])
        g12 = sb("g12", [P, NT, K2])
        rsel = sb("rsel", [P, TC, K2, E])
        rankf = sb("rankf", [P, 2, TC * K2])
        slot = sb("slot", [P, NT * K2], i32)
        pads_at = sb("pads_at", [1, E], i32)
        pad_rows = sb("pad_rows", [P, W])
        ntl = sb("ntl", [P, E])
        cmp = sb("cmp", [P, E * E])
        off = sb("off", [P, E])
        endt = sb("endt", [P, E])
        past = sb("past", [P, E])
        within = sb("within", [P, E])
        start = sb("start_", [P, E])
        junk_e = sb("junk_e", [P, 2, E])
        row_bank = sb("row_bank", [P, 2])
        tile_row = sb("tile_row", [1, Q], i32)
        bank = sb("bank", [1, Q + DEPTH], i32)
        dst = sb("dst", [P, Q], i32)
        xg = sb("xg", [P, DEPTH, W])
        xt = sb("xt", [D, 2, P])
        yo = sb("yo", [P, DEPTH, D])
        first = sb("first", [P, 1])
        sent = sb("sent", [P, 1])
        w1_now = leaky_r
        hid = leaky_l[:, :, :].rearrange("p k (c t) -> p k c t", c=FC)
        x1 = x1_rows[:, :, 0:D]
        ya, yb, res = h_sb, ht_sb[:, :].rearrange("p (t d) -> p t d", d=D), h_beta

        bk = [ctx.enter_context(nc.psum_tensor(f"bank{i}", [P, 512], f32)) for i in range(8)]
        ps_fr, ps_fl, ps_sr, ps_row, ps_g, ps_mix, ps_rt = bk[0:2], bk[2], bk[3], bk[4], bk[5], bk[6], bk[7]
        ps_sl, ps_stat = ps_row[:, 0:32], ps_row[:, 32:64]
        ps_lg, ps_rank, ps_count = ps_rt[:, 0:64], ps_rt[:, 128:208], ps_rt[:, 192:208]
        ps_tiles = bk[3]
        ps_h, ps_x, ps_y = (bk[0:2], bk[2:4]), (bk[4], bk[7]), bk[5:7]

        par0_in, par_in, con0_in, con_in = sem("par0_in"), sem("par_in"), sem("con0_in"), sem("con_in")
        h_in = [sem(f"h_in{j}") for j in range(NCH)]
        ht_in = [sem(f"ht_in{j}") for j in range(NCH)]
        w_in, b2_in = sem("w_in"), sem("b2_in")
        ones_ready, blocks_ready, before_ready = sem("ones_ready"), sem("blocks_ready"), sem("before_ready")
        hbeta_ready, tags_ready = sem("hbeta_ready"), sem("tags_ready")
        dve_link, pool_link, tag_link = sem("dve_link"), sem("pool_link"), sem("tag_link")
        fr_ready, fl_ready = sem("fr_ready"), sem("fl_ready")
        low_r_ready, pos_l_ready = sem("low_r_ready"), sem("pos_l_ready")
        leaky_r_ready, leaky_l_ready = sem("leaky_r_ready"), sem("leaky_l_ready")
        sr_ready, negmax_ready, col_ready, csumd_ready = (
            sem("sr_ready"), sem("negmax_ready"), sem("col_ready"), sem("csumd_ready"))
        sl_ready, g_ready, g_copied = sem("sl_ready"), sem("g_ready"), sem("g_copied")
        d1_ready, row_ready = sem("d1_ready"), sem("row_ready")
        scale_ready, scale_t_ready, scale_t_copied = sem("scale_ready"), sem("scale_t_ready"), sem("scale_t_copied")
        fh_ready, y_ready = sem("fh_ready"), sem("y_ready")
        mv_ready = [sem(f"mv_ready{n}") for n in range(3)]
        rstd_ready = [sem(f"rstd_ready{n}") for n in range(3)]
        yn_ready, z_ready, x1_ready = sem("yn_ready"), sem("z_ready"), sem("x1_ready")
        x1t_ready, x1t_copied = sem("x1t_ready"), sem("x1t_copied")
        lg_ready, both_ready, rank_ready, rank_read = (
            sem("lg_ready"), sem("both_ready"), sem("rank_ready"), sem("rank_read"))
        exin_ready, exo_ready = sem("exin_ready"), sem("exo_ready")
        slot_ready, dispatched, pads_at_ready, pads_ready, pads_out = (
            sem("slot_ready"), sem("dispatched"), sem("pads_at_ready"), sem("pads_ready"), sem("pads_out"))
        row_bank_ready, tiles_turned, tiles_ready = sem("row_bank_ready"), sem("tiles_turned"), sem("tiles_ready")
        x_in = [sem(f"x_in{k}") for k in range(DEPTH)]
        scattered = [sem(f"scattered{k}") for k in range(DEPTH)]
        xt_done, xt_copied, dst_ready = sem("xt_done"), sem("xt_copied"), sem("dst_ready")
        w1_ready, up_low, up_high = sem("w1_ready"), sem("up_low"), sem("up_high")
        relu_dve, relu_act = sem("relu_dve"), sem("relu_act")
        down_done, yo_ready = sem("down_done"), sem("yo_ready")
        y_in = [sem(f"y_in{j}") for j in range(NCH)]
        y1_scaled, y1_added, res_ready, out_done = sem("y1_scaled"), sem("y1_added"), sem("res_ready"), sem("out_done")

        block = ctx.enter_context(nc.Block())

        h_v = h.rearrange("b (p u) d -> p b (u d)", u=2)
        out_v = out.rearrange("b (p u) d -> p b (u d)", u=2)
        yb_v = y_rows[0:TOK, :].rearrange("(b p u) d -> p b (u d)", p=P, u=2)
        ya_v = y_rows[TOK:2 * TOK, :].rearrange("(b p u) d -> p b (u d)", p=P, u=2)

        def by_batch(t, j):
            return t[:, TC * j:TC * (j + 1), :].rearrange("p (b u) d -> p b (u d)", u=2)

        def tiles(j):
            return slice(TC * j, TC * (j + 1))

        def by_tile(a):
            return a[:, :].rearrange("p (t d) -> p t d", t=TC)

        def loop(engine, step):
            full = Q // DEPTH
            for k in range(DEPTH):
                step(k, k, 0)
            with engine.Fori(1, full) as i:
                for k in range(DEPTH):
                    step(DEPTH * i + k, k, i)
            for q in range(DEPTH * full, Q):
                step(q, q % DEPTH, full)

        def known(q):
            return isinstance(q, int)

        def wave(stages):
            for r in range(NCH + len(stages) - 1):
                for k in reversed(range(len(stages))):
                    if stages[k] is not None and 0 <= r - k < NCH:
                        stages[k](r - k)

        @block.sync
        def _(sp):
            sp.dma_start(par0[:, :], first_params[:, :]).then_inc(par0_in, 16)
            for j in range(NCH):
                sp.dma_start(ht_sb[:, j * CW:(j + 1) * CW], h_t[:, j * CW:(j + 1) * CW]).then_inc(ht_in[j], 16)
            for j in range(NCH):
                sp.dma_start(by_batch(h_sb, j), h_v[:, 2 * j:2 * j + 2, :]).then_inc(h_in[j], 16)
            for e in range(0, E, 4):
                sp.dma_start(w1_sb[:, e * F:(e + 4) * F], w1[:, e * F:(e + 4) * F]).then_inc(w_in, 16)
                sp.dma_start(w2_sb[:, e * F:(e + 4) * F], w2[:, e * F:(e + 4) * F]).then_inc(w_in, 16)
            sp.dma_start(b2_sb[:, :], b2.partition_broadcast(P)).then_inc(b2_in, 16)
            sp.wait_ge(pads_ready, 1)
            sp.dma_start(x_rows[E * REGION:E * REGION + P, :], pad_rows[:, :]).then_inc(pads_out, 16)
            sp.wait_ge(pads_at_ready, 1)
            for e in range(E):
                at = sp.value_load(pads_at[0:1, e:e + 1], min_val=e * REGION, max_val=e * REGION + TOK)
                sp.dma_start(x_rows[bass.ds(at, P), :], pad_rows[:, :]).then_inc(pads_out, 16)
            sp.wait_ge(tiles_ready, 1)
            sp.wait_ge(dispatched, 16 * NT * K2)
            sp.wait_ge(pads_out, 16 * (E + 1))

            def fetch(q, k, i):
                at = sp.value_load(tile_row[0:1, bass.ds(q, 1)], min_val=0, max_val=E * REGION)
                if not known(q) or q >= DEPTH:
                    sp.wait_ge(xt_done, q - DEPTH + 1)
                    sp.wait_ge(dst_ready, q - DEPTH + 1)
                sp.dma_start(xg[:, k, :], x_rows[bass.ds(at, P), :]).then_inc(x_in[k], 16)

            loop(sp, fetch)
            for k in range(DEPTH):
                sp.wait_ge(scattered[k], 16 * len(range(k, Q, DEPTH)))
            for j in range(NCH):
                sp.dma_start(by_batch(ya, j), ya_v[:, 2 * j:2 * j + 2, :]).then_inc(y_in[j], 16)
                sp.dma_start(by_batch(yb, j), yb_v[:, 2 * j:2 * j + 2, :]).then_inc(y_in[j], 16)
            for j in range(NCH):
                sp.wait_ge(res_ready, j + 1)
                sp.dma_start(out_v[:, 2 * j:2 * j + 2, :], by_batch(res, j)).then_inc(out_done, 16)
            sp.wait_ge(out_done, 16 * NCH)

        @block.scalar
        def _(act):
            act.dma_start(con0[:, :], first_consts[:, :]).then_inc(con0_in, 16)
            act.dma_start(con[:, :], consts[:, :]).then_inc(con_in, 16)
            act.dma_start(par[:, :], params[:, :]).then_inc(par_in, 16)

            def project(j):
                s = j % 2
                act.wait_ge(fr_ready, j + 1)
                if j >= 2:
                    act.wait_ge(sr_ready, j - 1)
                nc.scalar.activation(leaky_r[:, s, :], ps_fr[s][:, :], ACT.Copy, scale=0.01).then_inc(low_r_ready, 1)
                act.wait_ge(fl_ready, j + 1)
                if j >= 2:
                    act.wait_ge(sl_ready, j - 1)
                nc.scalar.activation(neg_l[:, s, :], ps_fl[:, :], ACT.Relu, scale=-0.01)
                nc.scalar.activation(leaky_l[:, s, :], ps_fl[:, :], ACT.Relu).then_inc(pos_l_ready, 1)

            def attend(j):
                s = j % 2
                act.wait_ge(negmax_ready, j + 1)
                if j >= 2:
                    act.wait_ge(csumd_ready, j - 1)
                for b in range(2):
                    nc.scalar.activation(col[:, s, b * N:(b + 1) * N], ps_sr[:, b * N:(b + 1) * N], ACT.Exp,
                                         bias=stat[:, j, b:b + 1],
                                         accum_out=stat[:, j, 2 + b:3 + b]).then_inc(col_ready, 1)

            def weigh(j):
                s = j % 2
                act.wait_ge(g_ready, j + 1)
                if j >= 2:
                    act.wait_ge(fh_ready, j - 1)
                nc.scalar.activation(g_sb[:, s, :, :].rearrange("h b d -> h (b d)"), ps_g[0:H, 0:2 * D],
                                     ACT.Copy).then_inc(g_copied, 1)
                act.wait_ge(d1_ready, j + 1)
                nc.scalar.activation(row[:, :], d1[:, :], ACT.Exp).then_inc(row_ready, 1)

            def mix(j):
                act.wait_ge(scale_t_ready, j + 1)
                nc.scalar.activation(scale_t[:, j % 2, :], ps_mix[0:H, :], ACT.Copy).then_inc(scale_t_copied, 1)

            def normalise(n, dst_, x, j, done):
                act.wait_ge(rstd_ready[n], j + 1)
                for t in range(TC):
                    ins = nc.scalar.activation(dst_[:, TC * j + t, :], x[:, TC * j + t, :], ACT.Identity,
                                               scale=rstd[:, n, j, t:t + 1], bias=shift[:, n, j, t:t + 1])
                ins.then_inc(done, 1)

            def norm1(j):
                normalise(0, x1, x1, j, yn_ready)

            def norm2(j):
                normalise(1, x1, x1, j, x1_ready)

            def logits(j):
                act.wait_ge(x1t_ready, j + 1)
                nc.scalar.activation(x1t[:, j % 2, :], ps_rt[:, :], ACT.Copy).then_inc(x1t_copied, 1)
                act.wait_ge(exin_ready, j + 1)
                nc.scalar.activation(exo[:, tiles(j), :], exin[:, tiles(j), :], ACT.Exp).then_inc(exo_ready, 1)

            wave([project, attend, weigh, mix, norm1, norm2, logits, None])

            held = [act.alloc_register(f"act_bank{k}") for k in range(2)]

            def load_w1(q, k):
                act.reg_load(held[k % 2], bank[0:1, bass.ds(q, 1)])
                e = act.snap(held[k % 2], min_val=0, max_val=E - 1)
                nc.scalar.activation(w1_now[:, k % 2, :], w1_sb[:, bass.ds(e * F, F)], ACT.Copy).then_inc(w1_ready, 1)

            def relu_high(q, k):
                e = act.snap(held[k % 2], min_val=0, max_val=E - 1)
                act.wait_ge(up_high, q + 1)
                if not known(q) or q >= 2:
                    act.wait_ge(down_done, q - 1)
                for c in range(FC // 2, FC):
                    ins = nc.scalar.activation(hid[:, k % 2, c, :],
                                               ps_h[k % 2][1][:, (c % 2) * P:(c % 2 + 1) * P], ACT.Relu,
                                               bias=views["b1_t"][:, bass.ds(e * FC + c, 1)])
                ins.then_inc(relu_act, 1)

            act.wait_ge(w_in, 16 * E // 2)
            act.wait_ge(tiles_ready, 1)
            load_w1(0, 0)

            def step(q, k, i):
                if not known(q) or q + 1 < Q:
                    load_w1(q + 1, k + 1)
                relu_high(q, k)

            loop(act, step)

            for j in range(NCH):
                act.wait_ge(y_in[j], 32)
                for t in range(TC * j, TC * (j + 1)):
                    ins = nc.scalar.activation(ya[:, t, :], ya[:, t, :], ACT.Copy, scale=g12[:, t, 0:1])
                ins.then_inc(y1_scaled, 1)
                if j:
                    normalise(2, res, ya, j - 1, res_ready)
            normalise(2, res, ya, NCH - 1, res_ready)

        @block.gpsimd
        def _(pool):
            links = [0]

            def link(ins):
                links[0] += 1
                ins.then_inc(pool_link, 1)
                pool.wait_ge(pool_link, links[0])

            nc.gpsimd.memset(ones[:, :], 1.0)
            nc.gpsimd.memset(ones_bf[:, :], 1.0).then_inc(ones_ready, 1)
            nc.gpsimd.memset(pad_rows[:, 0:D], 0.0)
            nc.gpsimd.memset(x1_rows[:, :, D + 2:D + 3], 0.0)
            pool.wait_ge(con_in, 16)
            nc.gpsimd.tensor_copy(pad_rows[:, D:W], views["pad_row"]).then_inc(pads_ready, 1)
            nc.gpsimd.tensor_copy(x1_rows[:, :, D:D + 1], views["token"].unsqueeze(2)).then_inc(tags_ready, 1)

            def rsqrt(n, j):
                pool.wait_ge(mv_ready[n], j + 1)
                nc.gpsimd.tensor_scalar(shift[:, n, j, :], mv[:, n, j, :, 0], -1.0, None, ALU.mult)
                link(nc.gpsimd.tensor_scalar(ve[:, n, j, :], mv[:, n, j, :, 1], LN_EPS, None, ALU.add))
                link(nc.gpsimd.tensor_tensor(rstd[:, n, j, :], ve[:, n, j, :], views["minus_half"], ALU.pow))
                nc.gpsimd.tensor_tensor(shift[:, n, j, :], shift[:, n, j, :], rstd[:, n, j, :],
                                        ALU.mult).then_inc(rstd_ready[n], 1)

            def project(j):
                s = j % 2
                pool.wait_ge(pos_l_ready, j + 1)
                nc.gpsimd.tensor_tensor(leaky_l[:, s, :], leaky_l[:, s, :], neg_l[:, s, :],
                                        ALU.subtract).then_inc(leaky_l_ready, 1)
                if j == 0:
                    pool.wait_ge(par_in, 16)
                    pool.wait_ge(con_in, 16)
                pool.wait_ge(h_in[j], 16)
                nc.gpsimd.tensor_tensor(h_beta[:, tiles(j), :], h_sb[:, tiles(j), :],
                                        views["beta"].unsqueeze(1).to_broadcast([P, TC, D]),
                                        ALU.add).then_inc(hbeta_ready, 1)

            def mix(j):
                rsqrt(0, j)

            def norm1(j):
                pool.wait_ge(yn_ready, j + 1)
                link(nc.gpsimd.tensor_tensor(x1[:, tiles(j), :], x1[:, tiles(j), :],
                                             views["gamma"].unsqueeze(1).to_broadcast([P, TC, D]), ALU.mult))
                pool.wait_ge(hbeta_ready, j + 1)
                nc.gpsimd.tensor_tensor(x1[:, tiles(j), :], x1[:, tiles(j), :], h_beta[:, tiles(j), :],
                                        ALU.add).then_inc(z_ready, 1)

            def norm2(j):
                rsqrt(1, j)

            def dispatch(j):
                pool.wait_ge(x1_ready, j + 1)
                pool.wait_ge(tags_ready, 1)
                pool.wait_ge(slot_ready, j + 1)
                for t in range(TC * j, TC * (j + 1)):
                    for c in range(K2):
                        nc.gpsimd.indirect_dma_start(
                            x_rows[:, :], bass.IndirectOffsetOnAxis(ap=slot[:, K2 * t + c:K2 * t + c + 1], axis=0),
                            x1_rows[:, t, :], None).then_inc(dispatched, 16)

            wave([project, None, None, mix, norm1, norm2, None, dispatch])

            for q in range(Q):
                pool.wait_ge(yo_ready, q + 1)
                nc.gpsimd.indirect_dma_start(y_rows[:, :], bass.IndirectOffsetOnAxis(ap=dst[:, q:q + 1], axis=0),
                                             yo[:, q % DEPTH, :], None).then_inc(scattered[q % DEPTH], 16)

            for j in range(NCH):
                pool.wait_ge(y1_scaled, j + 1)
                nc.gpsimd.tensor_tensor(ya[:, tiles(j), :], ya[:, tiles(j), :], x1[:, tiles(j), :],
                                        ALU.add).then_inc(y1_added, 1)
                if j:
                    rsqrt(2, j - 1)
            rsqrt(2, NCH - 1)

        @block.vector
        def _(dve):
            links = [0]

            def link(ins):
                links[0] += 1
                ins.then_inc(dve_link, 1)
                dve.wait_ge(dve_link, links[0])

            dve.wait_ge(par0_in, 16)
            dve.wait_ge(con0_in, 16)
            nc.vector.tensor_scalar(att_r_blk[:, :], views["same_head"], views["att_r"], None, ALU.mult)
            nc.vector.tensor_scalar(att_l_blk[:, :], views["head_of"], views["att_l"], None,
                                    ALU.mult).then_inc(blocks_ready, 1)

            def project(j):
                s = j % 2
                dve.wait_ge(low_r_ready, j + 1)
                nc.vector.tensor_tensor(leaky_r[:, s, :], ps_fr[s][:, :], leaky_r[:, s, :],
                                        ALU.max).then_inc(leaky_r_ready, 1)
                if j == 0:
                    dve.wait_ge(con_in, 16)
                    nc.vector.tensor_copy(before_bf[:, :], views["before"]).then_inc(before_ready, 1)

            def attend(j):
                s = j % 2
                dve.wait_ge(sr_ready, j + 1)
                nc.vector.tensor_reduce(stat[:, j, 0:2], ps_sr[:, :].rearrange("p (b n) -> p b n", b=2), AX,
                                        ALU.max, negate=True).then_inc(negmax_ready, 1)
                for b in range(2):
                    dve.wait_ge(col_ready, 2 * j + b + 1)
                    ins = nc.vector.scalar_tensor_tensor(junk[:, b, :], col[:, s, b * N:(b + 1) * N], 1.0,
                                                         ps_fr[s][:, b * N:(b + 1) * N], ALU.mult, ALU.mult,
                                                         accum_out=csum[:, j, b:b + 1])
                link(ins)
                if j >= 2:
                    dve.wait_ge(g_ready, j - 1)
                nc.vector.tensor_tensor(csumd[:, s, :, :], views["head_of"].unsqueeze(1).to_broadcast([D, 2, H]),
                                        csum[:, j, :].unsqueeze(2).to_broadcast([D, 2, H]), ALU.mult)
                nc.vector.tensor_tensor(statd[:, s, :, :], views["head_first"].unsqueeze(1).to_broadcast([D, 4, H]),
                                        stat[:, j, :].unsqueeze(2).to_broadcast([D, 4, H]),
                                        ALU.mult).then_inc(csumd_ready, 1)

            def weigh(j):
                s = j % 2
                dve.wait_ge(sl_ready, j + 1)
                link(nc.vector.tensor_copy(stat_tok[:, s, :, :].rearrange("p k h -> p (k h)"), ps_stat))

                def per_tile(a):
                    return a.unsqueeze(2).to_broadcast([P, 2, 2, H])

                def quad(a):
                    return a.rearrange("p (b u h) -> p b u h", b=2, u=2)

                negr, tot = per_tile(stat_tok[:, s, 0:2, :]), per_tile(stat_tok[:, s, 2:4, :])
                link(nc.vector.tensor_tensor(quad(rowmax[:, :]), quad(ps_sl), negr, ALU.subtract))
                link(nc.vector.tensor_tensor(d0[:, :], ps_sl, rowmax[:, :], ALU.subtract))
                nc.vector.tensor_tensor(quad(d1[:, :]), quad(d0[:, :]), negr, ALU.subtract).then_inc(d1_ready, 1)
                dve.wait_ge(row_ready, j + 1)
                link(nc.vector.tensor_tensor(quad(den[:, :]), quad(row[:, :]), tot, ALU.mult))
                link(nc.vector.reciprocal(rden[:, :], den[:, :]))
                nc.vector.tensor_tensor(scale[:, s, :, :].rearrange("p t h -> p (t h)"), row[:, :], rden[:, :],
                                        ALU.mult).then_inc(scale_ready, 1)

            def moments(n, x, j):
                for t in range(TC):
                    ins = nc.vector.bn_stats(bst[:, t, :], x[:, TC * j + t, :])
                link(ins)
                for t in range(TC):
                    ins = nc.vector.bn_aggr(mv[:, n, j, t, :], bst[:, t, :])
                ins.then_inc(mv_ready[n], 1)

            def mix(j):
                dve.wait_ge(h_in[j], 16)
                dve.wait_ge(fh_ready, j + 1)
                nc.vector.tensor_tensor(x1[:, tiles(j), :], by_tile(ps_mix), h_sb[:, tiles(j), :],
                                        ALU.add).then_inc(y_ready, 1)
                dve.wait_ge(y_ready, j + 1)
                moments(0, x1, j)

            def norm2(j):
                dve.wait_ge(z_ready, j + 1)
                moments(1, x1, j)

            def logits(j):
                T = tiles(j)
                if j == 0:
                    dve.wait_ge(par_in, 16)
                dve.wait_ge(lg_ready, j + 1)
                link(nc.vector.tensor_tensor(lg[:, T, :], ps_lg.rearrange("p (t e) -> p t e", t=TC),
                                             views["gate_b"].unsqueeze(1).to_broadcast([P, TC, E]), ALU.add))
                for t in range(TC * j, TC * (j + 1)):
                    ins = nc.vector.max(top[:, t, :], lg[:, t, :])
                link(ins)
                for t in range(TC * j, TC * (j + 1)):
                    ins = nc.vector.max_index(topi[:, t, :], top[:, t, :], lg[:, t, :])
                link(ins)
                link(nc.vector.tensor_tensor(
                    pick[:, T, :, :], views["iota_e"].unsqueeze(1).unsqueeze(1).to_broadcast([P, TC, K2, E]),
                    topi[:, T, 0:K2].unsqueeze(3).to_broadcast([P, TC, K2, E]), ALU.is_equal))
                nc.vector.tensor_tensor(both[:, T, :], pick[:, T, 0, :], pick[:, T, 1, :],
                                        ALU.add).then_inc(both_ready, 1)
                nc.vector.tensor_tensor(exin[:, T, 0:E], lg[:, T, :], top[:, T, 0:1].to_broadcast([P, TC, E]),
                                        ALU.subtract)
                nc.vector.tensor_tensor(exin[:, T, E:E + 1], top[:, T, 1:2], top[:, T, 0:1],
                                        ALU.subtract).then_inc(exin_ready, 1)
                nc.vector.tensor_copy(x1_rows[:, T, D + 1:D + 2], topi[:, T, 0:1])
                dve.wait_ge(rank_ready, j + 1)
                nc.vector.tensor_tensor(
                    rsel[:, :, :, :], pick[:, T, :, :],
                    ps_rank[:, 0:TC * E].rearrange("p (t e) -> p t e", t=TC).unsqueeze(2)
                    .to_broadcast([P, TC, K2, E]), ALU.mult).then_inc(rank_read, 1)
                if j == NCH - 1:
                    nc.vector.tensor_tensor(pads_at[:, :], ps_count[0:1, :], views["region"][0:1, :],
                                            ALU.add).then_inc(pads_at_ready, 1)
                    link(nc.vector.tensor_tensor(by_bank(cmp), by_bank(views["tile_floor"]),
                                                 ps_count.unsqueeze(2).to_broadcast([P, E, E]), ALU.is_lt))

            def by_bank(a):
                return a[:, :].rearrange("p (e k) -> p e k", e=E)

            def place(j):
                T = tiles(j)
                T2 = slice(TC * K2 * j, TC * K2 * (j + 1))
                dve.wait_ge(rank_read, j + 1)
                ranks = rankf[:, j % 2, :]
                link(nc.vector.tensor_reduce(ranks, rsel[:, :, :, :].rearrange("p t k e -> p (t k) e"), AX, ALU.add))
                nc.vector.scalar_tensor_tensor(slot[:, T2].rearrange("p (t k) -> p t k", k=K2), topi[:, T, 0:K2],
                                               float(REGION), ranks.rearrange("p (t k) -> p t k", k=K2),
                                               ALU.mult, ALU.add).then_inc(slot_ready, 1)
                dve.wait_ge(exo_ready, j + 1)
                link(nc.vector.tensor_reduce(esum[:, T], exo[:, T, 0:E], AX, ALU.add))
                link(nc.vector.reciprocal(g12[:, T, 0], esum[:, T]))
                link(nc.vector.tensor_tensor(g12[:, T, 1], exo[:, T, E], g12[:, T, 0], ALU.mult))

            wave([project, attend, weigh, mix, None, norm2, logits, place])

            link(nc.vector.tensor_reduce(ntl[:, :], by_bank(cmp), AX, ALU.add))
            link(nc.vector.tensor_tensor(by_bank(cmp), by_bank(views["bank_before"]),
                                         ntl[:, :].unsqueeze(1).to_broadcast([P, E, E]), ALU.mult))
            link(nc.vector.tensor_reduce(off[:, :], by_bank(cmp), AX, ALU.add))
            nc.vector.tensor_scalar(start[:, :], off[:, :], -1.0, None, ALU.mult)
            link(nc.vector.tensor_tensor(endt[:, :], off[:, :], ntl[:, :], ALU.add))
            nc.vector.tensor_tensor(start[:, :], start[:, :], views["start"], ALU.add)
            link(nc.vector.tensor_scalar(past[:, :], endt[:, :], views["tile"], None, ALU.is_le))
            link(nc.vector.scalar_tensor_tensor(within[:, :], off[:, :], views["tile"], past[:, :], ALU.is_le,
                                                ALU.subtract))
            nc.vector.scalar_tensor_tensor(junk_e[:, 0, :], start[:, :], 1.0, within[:, :], ALU.mult, ALU.mult,
                                           accum_out=row_bank[:, 0:1])
            nc.vector.scalar_tensor_tensor(junk_e[:, 1, :], views["iota_e"], 1.0, within[:, :], ALU.mult, ALU.mult,
                                           accum_out=row_bank[:, 1:2]).then_inc(row_bank_ready, 1)
            dve.wait_ge(tiles_turned, 1)
            nc.vector.tensor_scalar(tile_row[:, :], ps_tiles[0:1, 0:Q], float(E * REG_T), float(P), ALU.add, ALU.mult)
            nc.vector.tensor_copy(bank[:, 0:Q], ps_tiles[0:1, Q:2 * Q]).then_inc(tiles_ready, 1)

            held = [dve.alloc_register(f"dve_bank{k}") for k in range(DEPTH)]

            def copy_xt(q, k):
                dve.wait_ge(xt_done, q + 1)
                nc.vector.tensor_copy(xt[:, k % 2, :], ps_x[k % 2][:, 0:P]).then_inc(xt_copied, 1)

            def index(q, k):
                dve.reg_load(held[k % DEPTH], bank[0:1, bass.ds(q, 1)])
                e = dve.snap(held[k % DEPTH], min_val=0, max_val=E - 1)
                tag = xg[:, k % DEPTH, :]
                if not known(q) or q:
                    dve.wait_ge(dst_ready, q)
                nc.vector.tensor_scalar(first[:, :], tag[:, D + 1:D + 2], views["iota_e"][:, bass.ds(e, 1)],
                                        float(TOK), ALU.is_equal, ALU.mult)
                link_in_loop(nc.vector.scalar_tensor_tensor(sent[:, :], tag[:, D + 2:D + 3],
                                                            views["dump"][:, bass.ds(q, 1)],
                                                            tag[:, D:D + 1], ALU.mult, ALU.add), q)
                nc.vector.tensor_tensor(dst[:, bass.ds(q, 1)], first[:, :], sent[:, :], ALU.add).then_inc(dst_ready, 1)

            def link_in_loop(ins, q):
                ins.then_inc(tag_link, 1)
                dve.wait_ge(tag_link, q + 1)

            def relu_low(q, k):
                e = dve.snap(held[k % DEPTH], min_val=0, max_val=E - 1)
                dve.wait_ge(up_low, q + 1)
                for c in range(FC // 2):
                    ins = nc.vector.tensor_scalar(hid[:, k % 2, c, :], ps_h[k % 2][0][:, c * P:(c + 1) * P],
                                                  views["b1_t"][:, bass.ds(e * FC + c, 1)], 0.0, ALU.add, ALU.max)
                ins.then_inc(relu_dve, 1)

            def copy_y(q, k, i):
                e = dve.snap(held[k], min_val=0, max_val=E - 1)
                dve.wait_ge(down_done, q + 1)
                if not known(q) or q >= DEPTH:
                    dve.wait_ge(scattered[k], 16 * i)
                nc.vector.tensor_tensor(yo[:, k, :], ps_y[k % 2][:, 0:D], b2_sb[:, bass.ds(e * D, D)],
                                        ALU.add).then_inc(yo_ready, 1)

            dve.wait_ge(b2_in, 16)
            for q in range(2):
                copy_xt(q, q)
                index(q, q)
            relu_low(0, 0)

            def step(q, k, i):
                if not known(q) or q + 2 < Q:
                    copy_xt(q + 2, k + 2)
                    index(q + 2, k + 2)
                if not known(q) or q + 1 < Q:
                    relu_low(q + 1, k + 1)
                copy_y(q, k, i)

            loop(dve, step)

            for j in range(NCH):
                dve.wait_ge(y_in[j], 32)
                dve.wait_ge(y1_added, j + 1)
                for t in range(TC * j, TC * (j + 1)):
                    ins = nc.vector.scalar_tensor_tensor(ya[:, t, :], yb[:, t, :], g12[:, t, 1:2], ya[:, t, :],
                                                         ALU.mult, ALU.add)
                link(ins)
                moments(2, ya, j)

        @block.tensor
        def _(pe):
            ident = views["ident"]

            def project(j):
                s = j % 2
                if j == 0:
                    pe.wait_ge(par0_in, 16)
                pe.wait_ge(ht_in[j], 16)
                rows = ht_sb[:, j * CW:(j + 1) * CW]
                if j >= 2:
                    pe.wait_ge(csumd_ready, j - 1)
                nc.tensor.matmul(ps_fr[s][:, :], views["wr_t"], rows, start=True, stop=True).then_inc(fr_ready, 1)
                if j:
                    pe.wait_ge(pos_l_ready, j)
                nc.tensor.matmul(ps_fl[:, :], views["wl_t"], rows, start=True, stop=True).then_inc(fl_ready, 1)

            def attend(j):
                if j == 0:
                    pe.wait_ge(blocks_ready, 1)
                else:
                    pe.wait_ge(col_ready, 2 * j)
                pe.wait_ge(leaky_r_ready, j + 1)
                nc.tensor.matmul(ps_sr[:, :], att_r_blk[:, :], leaky_r[:, j % 2, :], start=True,
                                 stop=True).then_inc(sr_ready, 1)

            def weigh(j):
                s = j % 2
                if j == 0:
                    pe.wait_ge(ones_ready, 1)
                    pe.wait_ge(par_in, 16)
                else:
                    pe.wait_ge(d1_ready, j)
                    pe.wait_ge(g_copied, j)
                pe.wait_ge(leaky_l_ready, j + 1)
                for t in range(TC):
                    nc.tensor.matmul(ps_sl[:, H * t:H * (t + 1)], leaky_l[:, s, t * P:(t + 1) * P],
                                     att_l_blk[:, :], start=True, stop=True)
                pe.wait_ge(csumd_ready, j + 1)
                nc.tensor.matmul(ps_stat, ones[:, :], statd[:, s, :, :].rearrange("p k h -> p (k h)"), start=True,
                                 stop=True).then_inc(sl_ready, 1)
                for b in range(2):
                    ins = nc.tensor.matmul(ps_g[0:H, b * D:(b + 1) * D], csumd[:, s, b, :], views["wf_t"],
                                           start=True, stop=True)
                ins.then_inc(g_ready, 1)

            def mix(j):
                s = j % 2
                if j == 0:
                    pe.wait_ge(con_in, 16)
                else:
                    pe.wait_ge(y_ready, j)
                pe.wait_ge(scale_ready, j + 1)
                for t in range(TC):
                    ins = nc.tensor.transpose(ps_mix[0:H, t * P:(t + 1) * P], scale[:, s, t, :], ident)
                ins.then_inc(scale_t_ready, 1)
                pe.wait_ge(g_copied, j + 1)
                pe.wait_ge(scale_t_copied, j + 1)
                for t in range(TC):
                    ins = nc.tensor.matmul(ps_mix[:, t * P:(t + 1) * P], scale_t[:, s, t * P:(t + 1) * P],
                                           g_sb[:, s, t // 2, :], start=True, stop=True)
                ins.then_inc(fh_ready, 1)

            def logits(j):
                if j:
                    pe.wait_ge(rank_read, j)
                pe.wait_ge(x1_ready, j + 1)
                for t in range(TC):
                    ins = nc.tensor.transpose(ps_rt[:, t * P:(t + 1) * P], x1[:, TC * j + t, :], ident)
                ins.then_inc(x1t_ready, 1)
                pe.wait_ge(x1t_copied, j + 1)
                for t in range(TC):
                    ins = nc.tensor.matmul(ps_lg[:, E * t:E * (t + 1)], x1t[:, j % 2, t * P:(t + 1) * P],
                                           views["gate_w"], start=True, stop=True)
                ins.then_inc(lg_ready, 1)
                if j == 0:
                    pe.wait_ge(before_ready, 1)
                pe.wait_ge(both_ready, j + 1)
                for t in range(TC * (j + 1)):
                    lo = max(t - TC * j + 1, 0)
                    nc.tensor.matmul(ps_rank[:, E * lo:E * (TC + 1)], ones_bf[:, :],
                                     both[:, t, :].unsqueeze(1).to_broadcast([P, TC + 1 - lo, E]),
                                     start=t == 0, stop=False, skip_group_check=True)
                for t in range(TC):
                    ins = nc.tensor.matmul(ps_rank[:, E * t:E * (t + 1)], before_bf[:, :], both[:, TC * j + t, :],
                                           start=False, stop=t == TC - 1, skip_group_check=True)
                ins.then_inc(rank_ready, 1)

            wave([project, attend, weigh, mix, None, None, logits, None])

            pe.wait_ge(row_bank_ready, 1)
            for c in range(2):
                ins = nc.tensor.matmul(ps_tiles[0:1, c * Q:(c + 1) * Q], row_bank[:, c:c + 1], ident[:, 0:Q],
                                       start=True, stop=True)
            ins.then_inc(tiles_turned, 1)

            held = [pe.alloc_register(f"pe_bank{k}") for k in range(2)]

            def turn_x(q, k, i):
                pe.wait_ge(x_in[k % DEPTH], 16 * (i + 1))
                nc.tensor.transpose(ps_x[k % 2][:, 0:P], xg[:, k % DEPTH, 0:D], ident).then_inc(xt_done, 1)

            def up(q, k):
                pe.wait_ge(xt_copied, q + 1)
                pe.wait_ge(w1_ready, q + 1)
                for c in range(FC):
                    half = c // 2
                    ins = nc.tensor.matmul(ps_h[k % 2][half][:, (c % 2) * P:(c % 2 + 1) * P],
                                           w1_now[:, k % 2, c * P:(c + 1) * P], xt[:, k % 2, :], start=True,
                                           stop=True)
                    if c % 2:
                        ins.then_inc((up_low, up_high)[half], 1)

            def down(q, k):
                e = pe.snap(held[k % 2], min_val=0, max_val=E - 1)
                pe.wait_ge(relu_dve, q + 1)
                for c in range(FC):
                    if c == FC // 2:
                        pe.wait_ge(relu_act, q + 1)
                    ins = nc.tensor.matmul(ps_y[k % 2][:, 0:D], hid[:, k % 2, c, :],
                                           w2_sb[:, bass.ds(e * F + c * P, P)], start=c == 0, stop=c == FC - 1)
                ins.then_inc(down_done, 1)

            pe.wait_ge(w_in, 16 * E // 2)
            pe.wait_ge(tiles_ready, 1)
            turn_x(0, 0, 0)
            turn_x(1, 1, 0)
            up(0, 0)

            def step(q, k, i):
                if not known(q) or q + 2 < Q:
                    turn_x(q + 2, k + 2, i + (k + 2) // DEPTH)
                if not known(q) or q + 1 < Q:
                    up(q + 1, k + 1)
                pe.reg_load(held[k % 2], bank[0:1, bass.ds(q, 1)])
                down(q, k)

            loop(pe, step)


def kernel(L0_attn_h, L0_attn_Wl, L0_attn_Wr, L0_attn_att_l, L0_attn_att_r, L0_attn_Wf, L0_attn_ln_gamma,
           L0_attn_ln_beta, L0_ffn_Wr, L0_ffn_br, L0_ffn_W1, L0_ffn_b1, L0_ffn_W2, L0_ffn_b2):
    import concourse.bacc as bacc
    from concourse.bass_utils import run_bass_kernel_spmd

    a = [np.asarray(x) for x in (L0_attn_h, L0_attn_Wl, L0_attn_Wr, L0_attn_att_l, L0_attn_att_r, L0_attn_Wf,
                                 L0_attn_ln_gamma, L0_attn_ln_beta, L0_ffn_Wr, L0_ffn_br, L0_ffn_W1, L0_ffn_b1,
                                 L0_ffn_W2, L0_ffn_b2)]
    h, wl, wr, att_l, att_r, wf, gamma, beta, gw, gb, w1, b1, w2, b2 = a

    def rows(v):
        return np.broadcast_to(v.reshape(1, -1), (P, v.size))

    c0, c = shape_constants()
    ins = {
        "h": h,
        "h_t": h.reshape(B, P, 2, D).transpose(3, 0, 2, 1).reshape(D, TOK),
        "first_params": np.concatenate([wr.T, wl.T, np.tile(att_r.reshape(-1), H)[:, None],
                                        np.tile(att_l.reshape(-1), H)[:, None]], axis=1),
        "params": np.concatenate([wf.T, rows(gamma), rows(beta), gw, rows(gb),
                                  b1.reshape(E, FC, P).transpose(2, 0, 1).reshape(P, E * FC)], axis=1),
        "first_consts": c0,
        "consts": c,
        "w1": w1.transpose(1, 0, 2).reshape(D, E * F),
        "w2": w2.reshape(E, FC, P, D).transpose(2, 0, 1, 3).reshape(P, E * F),
        "b2": b2.reshape(E * D),
    }
    ins = {k: np.ascontiguousarray(v) for k, v in ins.items()}
    nc = bacc.Bacc("TRN2", target_bir_lowering=False, num_devices=1)
    aps = [nc.dram_tensor(k, v.shape, mybir.dt.from_np(v.dtype), kind="ExternalInput").ap() for k, v in ins.items()]
    out = nc.dram_tensor("out", (B, N, D), mybir.dt.float32, kind="ExternalOutput").ap()
    x_rows = nc.dram_tensor("x_rows", (XROWS, W), mybir.dt.float32, kind="Internal").ap()
    y_rows = nc.dram_tensor("y_rows", (YROWS, D), mybir.dt.float32, kind="Internal").ap()
    routed_block(nc, *aps, out, x_rows, y_rows)
    r = run_bass_kernel_spmd(nc, [ins], core_ids=[0])
    return r.results[0]["out"]
```

```python
import numpy as np
import concourse.bass as bass
from concourse import mybir
from contextlib import ExitStack

P = 128
B, N, D = 8, 256, 128
H, HD = 8, 16
E, F = 16, 512
TOK = B * N
NT = TOK // P
NCH = 4
TC = NT // NCH
CW = TC * P
FC = F // P
K2 = 2
Q = (TOK * K2 + E * (P - 1)) // P
LN_EPS = 1e-5
REGION = TOK + P
REG_T = REGION // P
XROWS = E * REGION + P
W = D + 3
DEPTH = 4
YROWS = K2 * TOK + Q * P


STAGES = (("project", 0), ("scores", 5.82), ("factors", 5.92), ("weigh", 8.96), ("scales", 10.96),
          ("turn", 12.46), ("mix", 15.87), ("norm1", 19.86), ("norm2", 22.79), ("turn_x1", 24.56),
          ("logits", 28.31), ("rank", 28.74), ("dispatch0", 31.76), ("dispatch1", 33.76), ("dispatch2", 35.76),
          ("dispatch3", 37.76))
STARTS = (0, 6.12, 14.12, 22.12)
ORDER = [(j, name) for _, j, name in sorted((STARTS[j] + at, j, name) for name, at in STAGES for j in range(NCH))]


def columns(widths):
    at, out = 0, {}
    for name, w in widths:
        out[name] = (at, at + w)
        at += w
    return out, at


PCOLS0, PW0 = columns([("wr_t", D), ("wl_t", D), ("att_r", 1), ("att_l", 1)])
PCOLS, PW = columns([("wf_t", D), ("gamma", D), ("beta", D), ("gate_w", E), ("gate_b", E)])
CCOLS0, CWID0 = columns([("same_head", D), ("head_of", H), ("head_first", H)])
CCOLS, CWID = columns([("ident", P), ("before", P), ("token", NT), ("iota_e", E), ("bank_no", P), ("dump", Q), ("pad_row", 3),
                       ("region", E), ("bank_before", E * E), ("tile_floor", E * E), ("tile", 1), ("start", E),
                       ("minus_half", TC)])


def shape_constants():
    c0, c = np.zeros((P, CWID0), np.float32), np.zeros((P, CWID), np.float32)

    def put(name, a):
        where, (lo, hi) = (c0, CCOLS0[name]) if name in CCOLS0 else (c, CCOLS[name])
        where[:, lo:hi] = a

    p = np.arange(P)[:, None]
    e = np.arange(E)
    put("same_head", p // HD == np.arange(D)[None] // HD)
    put("head_of", p // HD == np.arange(H)[None])
    put("head_first", p == HD * np.arange(H)[None])
    put("ident", p == np.arange(P)[None])
    put("before", p < np.arange(P)[None])
    put("token", N * (np.arange(NT)[None] // 2) + 2 * p + np.arange(NT)[None] % 2)
    put("iota_e", e[None])
    put("bank_no", p)
    put("dump", P * np.arange(Q)[None])
    put("pad_row", np.concatenate([K2 * TOK + p, np.full_like(p, -1), np.ones_like(p)], axis=1))
    put("region", REGION * e[None])
    put("bank_before", (e[None, :] < e[:, None]).reshape(1, -1))
    put("tile_floor", np.broadcast_to(P * e[None, :], (E, E)).reshape(1, -1))
    put("tile", p)
    put("start", REG_T * e[None] + p - E * REG_T)
    put("minus_half", -0.5)
    return c0, c


def routed_block(nc, h, h_t, first_params, params, first_consts, consts, w1, w2, b1, b2, out, x_rows, y_rows):
    f32, bf16, f16 = mybir.dt.float32, mybir.dt.bfloat16, mybir.dt.float16
    i32, u32 = mybir.dt.int32, mybir.dt.uint32
    ALU, ACT, AX = mybir.AluOpType, mybir.ActivationFunctionType, mybir.AxisListType.X
    ctx = ExitStack()
    with ctx:
        def sb(name, shape, dt=f32):
            return ctx.enter_context(nc.sbuf_tensor(name, shape, dt))

        def sem(name):
            return ctx.enter_context(nc.semaphore(name))

        par0, par, con0, con = sb("par0", [P, PW0]), sb("par", [P, PW]), sb("con0", [P, CWID0]), sb("con", [P, CWID])
        views = {}
        for t, cols in ((par0, PCOLS0), (par, PCOLS), (con0, CCOLS0), (con, CCOLS)):
            for name, (lo, hi) in cols.items():
                views[name] = t[:, lo:hi]
        h_sb = sb("h_sb", [P, NT, D])
        ht_sb = sb("ht_sb", [D, TOK])
        w1_sb = sb("w1_sb", [D, E * F])
        w2_sb = sb("w2_sb", [P, E * F])
        b1_sb = sb("b1_sb", [E, F])
        b2_sb = sb("b2_sb", [TC * E, TC, D])

        ones = sb("ones", [P, P])
        ones_bf = sb("ones_bf", [P, P], bf16)
        before_bf = sb("before_bf", [P, P], bf16)
        att_r_blk = sb("att_r_blk", [D, D])
        att_l_blk = sb("att_l_blk", [D, H])
        h_beta = sb("h_beta", [P, NT, D])
        gates = sb("gates", [P, 2, NT, E])
        gates_t = sb("gates_t", [TC * E, NCH, P])
        leaky_r = sb("leaky_r", [D, 2, CW])
        leaky_l = sb("leaky_l", [D, 2, CW])
        neg_l = sb("neg_l", [D, 2, CW])
        col = sb("col", [D, 2, CW])
        junk = sb("junk", [D, 2, N])
        stat = sb("stat", [D, NCH, 4])
        csum = sb("csum", [D, NCH, 2])
        statd = sb("statd", [D, 2, 4, H])
        csumd = sb("csumd", [D, 2, 2, H])
        stat_tok = sb("stat_tok", [P, 2, 4, H])
        rowmax = sb("rowmax", [P, 32])
        d0 = sb("d0", [P, 32])
        d1 = sb("d1", [P, 32])
        row = sb("row", [P, 32])
        den = sb("den", [P, 32])
        rden = sb("rden", [P, 32])
        scale = sb("scale", [P, 2, TC, H])
        g_sb = sb("g_sb", [H, 2, 2, D])
        scale_t = sb("scale_t", [H, 2, CW])
        bst = sb("bst", [P, TC, 6])
        mv = sb("mv", [P, 3, NCH, TC, 2])
        ve = sb("ve", [P, 3, NCH, TC])
        negmean = sb("negmean", [P, 3, NCH, TC])
        rstd = sb("rstd", [P, 3, NCH, TC])
        shift = sb("shift", [P, 3, NCH, TC])
        x1_rows = sb("x1_rows", [P, NT, W])
        x1t = sb("x1t", [D, 2, CW])
        lg = sb("lg", [P, NT, E])
        top = sb("top", [P, NT, 8])
        topi = sb("topi", [P, NT, 8], u32)
        pick = sb("pick", [P, NT, K2, E])
        both = sb("both", [P, NT, E], bf16)
        exin = sb("exin", [P, NT, E + 1])
        exo = sb("exo", [P, NT, E + 1])
        esum = sb("esum", [P, NT])
        g12 = sb("g12", [P, NT, K2])
        rsel = sb("rsel", [P, TC, K2, E])
        rankf = sb("rankf", [P, 2, TC * K2])
        slot = sb("slot", [P, NT * K2], i32)
        pads_at = sb("pads_at", [1, E], i32)
        pad_rows = sb("pad_rows", [P, W])
        ntl = sb("ntl", [P, E])
        cmp = sb("cmp", [P, E * E])
        off = sb("off", [P, E])
        endt = sb("endt", [P, E])
        past = sb("past", [P, E])
        within = sb("within", [P, E])
        start = sb("start_", [P, E])
        junk_e = sb("junk_e", [P, 2, E])
        row_bank = sb("row_bank", [P, 2])
        bank_hot = sb("bank_hot", [E, Q])
        by_q = sb("by_q", [P, FC + 1, Q])
        tile_row = sb("tile_row", [1, Q], i32)
        bank = sb("bank", [1, Q + DEPTH], i32)
        dst = sb("dst", [P, Q], i32)
        xg = sb("xg", [P, DEPTH, W])
        xt = sb("xt", [D, 2, P])
        yo = sb("yo", [P, DEPTH, D])
        first = sb("first", [P, 2])
        dump = sb("dump_", [P, 2])
        row_no = sb("row_no", [P, 2])
        w1_now = leaky_r
        hid = leaky_l[:, :, :].rearrange("p k (c t) -> p k c t", c=FC)
        base = h_beta
        x1 = x1_rows[:, :, 0:D]
        ya, yb, res = h_sb, ht_sb[:, :].rearrange("p (t d) -> p t d", d=D), h_beta

        bk = [ctx.enter_context(nc.psum_tensor(f"bank{i}", [P, 512], f32)) for i in range(8)]
        ps_fr, ps_fl, ps_sr, ps_row, ps_g, ps_mix, ps_rt = bk[0:2], bk[2], bk[3], bk[4], bk[5], bk[6], bk[7]
        ps_sl, ps_stat = ps_row[:, 0:32], ps_row[:, 32:64]
        ps_lg, ps_rank, ps_count = ps_rt[:, 0:64], ps_rt[:, 128:208], ps_rt[:, 192:208]
        ps_tiles, ps_byq, ps_gt, ps_bias = bk[3], bk[2], bk[1], bk[2:4]
        ps_h, ps_x, ps_y = (bk[0:2], bk[2:4]), (bk[4], bk[7]), bk[5:7]

        par0_in, par_in, con0_in, con_in = sem("par0_in"), sem("par_in"), sem("con0_in"), sem("con_in")
        h_in = [sem(f"h_in{j}") for j in range(NCH)]
        ht_in = [sem(f"ht_in{j}") for j in range(NCH)]
        w_in, b_in, b2_cleared = sem("w_in"), sem("b_in"), sem("b2_cleared")
        ones_ready, blocks_ready, before_ready = sem("ones_ready"), sem("blocks_ready"), sem("before_ready")
        hbeta_ready, tags_ready = sem("hbeta_ready"), sem("tags_ready")
        dve_link, pool_link, parts_link, row_no_link = (
            sem("dve_link"), sem("pool_link"), sem("parts_link"), sem("row_no_link"))
        fr_ready, fl_ready = sem("fr_ready"), sem("fl_ready")
        low_r_ready, pos_l_ready = sem("low_r_ready"), sem("pos_l_ready")
        leaky_r_ready, leaky_l_ready = sem("leaky_r_ready"), sem("leaky_l_ready")
        sr_ready, negmax_ready, col_ready, csumd_ready = (
            sem("sr_ready"), sem("negmax_ready"), sem("col_ready"), sem("csumd_ready"))
        sl_ready, g_ready, g_copied = sem("sl_ready"), sem("g_ready"), sem("g_copied")
        d1_ready, row_ready = sem("d1_ready"), sem("row_ready")
        scale_ready, scale_t_ready, scale_t_copied = sem("scale_ready"), sem("scale_t_ready"), sem("scale_t_copied")
        fh_ready, y_ready = sem("fh_ready"), sem("y_ready")
        mv_ready = [sem(f"mv_ready{n}") for n in range(3)]
        rstd_ready = [sem(f"rstd_ready{n}") for n in range(3)]
        centred, x1_low, x1_high = sem("centred"), sem("x1_low"), sem("x1_high")
        x1t_ready, x1t_copied = sem("x1t_ready"), sem("x1t_copied")
        lg_ready, both_ready, rank_ready, rank_read = (
            sem("lg_ready"), sem("both_ready"), sem("rank_ready"), sem("rank_read"))
        exin_ready, exo_ready = sem("exin_ready"), sem("exo_ready")
        slot_ready, dispatched, pads_at_ready, pads_ready, pads_out = (
            sem("slot_ready"), sem("dispatched"), sem("pads_at_ready"), sem("pads_ready"), sem("pads_out"))
        row_bank_ready, tiles_turned, tiles_ready = sem("row_bank_ready"), sem("tiles_turned"), sem("tiles_ready")
        bank_hot_ready, by_q_summed, by_q_ready = sem("bank_hot_ready"), sem("by_q_summed"), sem("by_q_ready")
        gates_ready, gates_turned, gates_t_ready, bias_ready, base_ready = (
            sem("gates_ready"), sem("gates_turned"), sem("gates_t_ready"), sem("bias_ready"), sem("base_ready"))
        x_in = [sem(f"x_in{k}") for k in range(DEPTH)]
        scattered = [sem(f"scattered{k}") for k in range(DEPTH)]
        xt_done, xt_copied, dst_ready = sem("xt_done"), sem("xt_copied"), sem("dst_ready")
        w1_ready, up_low, up_high = sem("w1_ready"), sem("up_low"), sem("up_high")
        relu_dve, relu_act = sem("relu_dve"), sem("relu_act")
        down_done, yo_ready = sem("down_done"), sem("yo_ready")
        ya_in = [sem(f"ya_in{j}") for j in range(NCH)]
        yb_in = [sem(f"yb_in{j}") for j in range(NCH)]
        y1_scaled, y2_added, y1_added, res_ready, last_halves, out_done = (
            sem("y1_scaled"), sem("y2_added"), sem("y1_added"), sem("res_ready"), sem("last_halves"), sem("out_done"))

        block = ctx.enter_context(nc.Block())

        h_v = h.rearrange("b (p u) d -> p b (u d)", u=2)
        out_v = out.rearrange("b (p u) d -> p b (u d)", u=2)
        yb_v = y_rows[0:TOK, :].rearrange("(b p u) d -> p b (u d)", p=P, u=2)
        ya_v = y_rows[TOK:2 * TOK, :].rearrange("(b p u) d -> p b (u d)", p=P, u=2)

        def by_batch(t, j):
            return t[:, TC * j:TC * (j + 1), :].rearrange("p (b u) d -> p b (u d)", u=2)

        def tiles(j):
            return slice(TC * j, TC * (j + 1))

        def by_tile(a):
            return a[:, :].rearrange("p (t d) -> p t d", t=TC)

        def loop(engine, step):
            full = Q // DEPTH
            for k in range(DEPTH):
                step(k, k, 0)
            with engine.Fori(1, full) as i:
                for k in range(DEPTH):
                    step(DEPTH * i + k, k, i)
            for q in range(DEPTH * full, Q):
                step(q, q % DEPTH, full)

        def known(q):
            return isinstance(q, int)

        def in_order(**parts):
            for j, name in ORDER:
                if name in parts:
                    parts[name](j)

        @block.sync
        def _(sp):
            sp.dma_start(par0[:, :], first_params[:, :]).then_inc(par0_in, 16)
            for j in range(NCH):
                sp.dma_start(ht_sb[:, j * CW:(j + 1) * CW], h_t[:, j * CW:(j + 1) * CW]).then_inc(ht_in[j], 16)
            for j in range(NCH):
                sp.dma_start(by_batch(h_sb, j), h_v[:, 2 * j:2 * j + 2, :]).then_inc(h_in[j], 16)
            for e in range(0, E, 4):
                sp.dma_start(w1_sb[:, e * F:(e + 4) * F], w1[:, e * F:(e + 4) * F]).then_inc(w_in, 16)
                sp.dma_start(w2_sb[:, e * F:(e + 4) * F], w2[:, e * F:(e + 4) * F]).then_inc(w_in, 16)
            sp.dma_start(b1_sb[:, :], b1[:, :]).then_inc(b_in, 16)
            sp.wait_ge(b2_cleared, 1)
            for t in range(TC):
                sp.dma_start(b2_sb[E * t:E * (t + 1), t, :], b2[:, :]).then_inc(b_in, 16)
            sp.wait_ge(pads_ready, 1)
            sp.dma_start(x_rows[E * REGION:E * REGION + P, :], pad_rows[:, :]).then_inc(pads_out, 16)
            sp.wait_ge(pads_at_ready, 1)
            for e in range(0, E, 2):
                at = sp.value_load(pads_at[0:1, e:e + 1], min_val=e * REGION, max_val=e * REGION + TOK)
                sp.dma_start(x_rows[bass.ds(at, P), :], pad_rows[:, :]).then_inc(pads_out, 16)
            sp.wait_ge(tiles_ready, 1)
            sp.wait_ge(dispatched, 16 * NT * K2)
            sp.wait_ge(pads_out, 16 * (E + 1))

            def fetch(q, k, i):
                at = sp.value_load(tile_row[0:1, bass.ds(q, 1)], min_val=0, max_val=E * REGION)
                if not known(q) or q >= DEPTH:
                    sp.wait_ge(xt_done, q - DEPTH + 1)
                    sp.wait_ge(dst_ready, q - DEPTH + 1)
                sp.dma_start(xg[:, k, :], x_rows[bass.ds(at, P), :]).then_inc(x_in[k], 16)

            loop(sp, fetch)
            for k in range(DEPTH):
                sp.wait_ge(scattered[k], 16 * len(range(k, Q, DEPTH)))
            for j in range(NCH):
                sp.dma_start(by_batch(ya, j), ya_v[:, 2 * j:2 * j + 2, :]).then_inc(ya_in[j], 16)
                sp.dma_start(by_batch(yb, j), yb_v[:, 2 * j:2 * j + 2, :]).then_inc(yb_in[j], 16)
            for j in range(NCH):
                sp.wait_ge(res_ready, j + 1)
                if j >= NCH - 2:
                    sp.wait_ge(last_halves, j - NCH + 3)
                sp.dma_start(out_v[:, 2 * j:2 * j + 2, :], by_batch(res, j)).then_inc(out_done, 16)
            sp.wait_ge(out_done, 16 * NCH)

        @block.scalar
        def _(act):
            act.dma_start(con0[:, :], first_consts[:, :]).then_inc(con0_in, 16)
            act.dma_start(con[:, :], consts[:, :]).then_inc(con_in, 16)
            act.dma_start(par[:, :], params[:, :]).then_inc(par_in, 16)

            def project(j):
                s = j % 2
                act.wait_ge(fr_ready, j + 1)
                if j >= 2:
                    act.wait_ge(sr_ready, j - 1)
                nc.scalar.activation(leaky_r[:, s, :], ps_fr[s][:, :], ACT.Copy, scale=0.01).then_inc(low_r_ready, 1)
                act.wait_ge(fl_ready, j + 1)
                if j >= 2:
                    act.wait_ge(sl_ready, j - 1)
                nc.scalar.activation(neg_l[:, s, :], ps_fl[:, :], ACT.Relu, scale=-0.01)
                nc.scalar.activation(leaky_l[:, s, :], ps_fl[:, :], ACT.Relu).then_inc(pos_l_ready, 1)

            def factors(j):
                s = j % 2
                act.wait_ge(negmax_ready, j + 1)
                if j >= 2:
                    act.wait_ge(csumd_ready, j - 1)
                for b in range(2):
                    nc.scalar.activation(col[:, s, b * N:(b + 1) * N], ps_sr[:, b * N:(b + 1) * N], ACT.Exp,
                                         bias=stat[:, j, b:b + 1],
                                         accum_out=stat[:, j, 2 + b:3 + b]).then_inc(col_ready, 1)

            def weigh(j):
                s = j % 2
                act.wait_ge(g_ready, j + 1)
                if j >= 2:
                    act.wait_ge(fh_ready, j - 1)
                nc.scalar.activation(g_sb[:, s, :, :].rearrange("h b d -> h (b d)"), ps_g[0:H, 0:2 * D],
                                     ACT.Copy).then_inc(g_copied, 1)

            def scales(j):
                act.wait_ge(d1_ready, j + 1)
                nc.scalar.activation(row[:, :], d1[:, :], ACT.Exp).then_inc(row_ready, 1)

            def turn(j):
                act.wait_ge(scale_t_ready, j + 1)
                nc.scalar.activation(scale_t[:, j % 2, :], ps_mix[0:H, :], ACT.Copy).then_inc(scale_t_copied, 1)

            def normalise(n, dst_, x, j, which, done):
                act.wait_ge(rstd_ready[n], j + 1)
                for t in which:
                    ins = nc.scalar.activation(dst_[:, TC * j + t, :], x[:, TC * j + t, :], ACT.Identity,
                                               scale=rstd[:, n, j, t:t + 1], bias=shift[:, n, j, t:t + 1])
                ins.then_inc(done, 1)

            def norm2(j):
                normalise(1, x1, x1, j, range(TC // 2, TC), x1_high)

            def turn_x1(j):
                act.wait_ge(x1t_ready, j + 1)
                nc.scalar.activation(x1t[:, j % 2, :], ps_rt[:, :], ACT.Copy).then_inc(x1t_copied, 1)

            def rank(j):
                act.wait_ge(exin_ready, j + 1)
                nc.scalar.activation(exo[:, tiles(j), :], exin[:, tiles(j), :], ACT.Exp).then_inc(exo_ready, 1)

            in_order(project=project, factors=factors, weigh=weigh, scales=scales, turn=turn, norm2=norm2,
                     turn_x1=turn_x1, rank=rank)

            act.wait_ge(pads_ready, 1)
            act.wait_ge(pads_at_ready, 1)
            for e in range(1, E, 2):
                at = act.value_load(pads_at[0:1, e:e + 1], min_val=e * REGION, max_val=e * REGION + TOK)
                act.dma_start(x_rows[bass.ds(at, P), :], pad_rows[:, :]).then_inc(pads_out, 16)

            held = [act.alloc_register(f"act_bank{k}") for k in range(2)]

            def load_w1(q, k):
                act.reg_load(held[k % 2], bank[0:1, bass.ds(q, 1)])
                e = act.snap(held[k % 2], min_val=0, max_val=E - 1)
                nc.scalar.activation(w1_now[:, k % 2, :], w1_sb[:, bass.ds(e * F, F)], ACT.Copy).then_inc(w1_ready, 1)

            def relu_high(q, k):
                act.wait_ge(up_high, q + 1)
                if not known(q) or q >= 2:
                    act.wait_ge(down_done, q - 1)
                for c in range(FC // 2, FC):
                    ins = nc.scalar.activation(hid[:, k % 2, c, :],
                                               ps_h[k % 2][1][:, (c % 2) * P:(c % 2 + 1) * P], ACT.Relu,
                                               bias=by_q[:, c, bass.ds(q, 1)])
                ins.then_inc(relu_act, 1)

            act.wait_ge(w_in, 16 * E // 2)
            act.wait_ge(tiles_ready, 1)
            load_w1(0, 0)
            act.wait_ge(by_q_ready, 1)

            def step(q, k, i):
                if not known(q) or q + 1 < Q:
                    load_w1(q + 1, k + 1)
                relu_high(q, k)

            loop(act, step)

            def scale_y1(j):
                act.wait_ge(ya_in[j], 16)
                for t in range(TC * j, TC * (j + 1)):
                    ins = nc.scalar.activation(ya[:, t, :], ya[:, t, :], ACT.Copy, scale=g12[:, t, 0:1])
                ins.then_inc(y1_scaled, 1)

            for j in range(NCH):
                scale_y1(j)
            for j in range(NCH):
                normalise(2, res, ya, j, range(TC // 2 if j >= NCH - 2 else 0, TC), res_ready)

        @block.gpsimd
        def _(pool):
            links = [0]

            def link(ins):
                links[0] += 1
                ins.then_inc(pool_link, 1)
                pool.wait_ge(pool_link, links[0])

            nc.gpsimd.memset(ones[:, :], 1.0)
            nc.gpsimd.memset(ones_bf[:, :], 1.0).then_inc(ones_ready, 1)
            nc.gpsimd.memset(b2_sb[:, :, :], 0.0).then_inc(b2_cleared, 1)
            nc.gpsimd.memset(pad_rows[:, 0:D], 0.0)
            nc.gpsimd.memset(x1_rows[:, :, D + 2:D + 3], 0.0)
            pool.wait_ge(con_in, 16)
            nc.gpsimd.tensor_copy(pad_rows[:, D:W], views["pad_row"]).then_inc(pads_ready, 1)
            nc.gpsimd.tensor_copy(x1_rows[:, :, D:D + 1], views["token"].unsqueeze(2)).then_inc(tags_ready, 1)

            def rsqrt(n, j):
                pool.wait_ge(mv_ready[n], j + 1)
                if n == 0:
                    nc.gpsimd.tensor_tensor(rstd[:, n, j, :], ve[:, n, j, :], views["minus_half"],
                                            ALU.pow).then_inc(rstd_ready[n], 1)
                    return
                link(nc.gpsimd.tensor_tensor(rstd[:, n, j, :], ve[:, n, j, :], views["minus_half"], ALU.pow))
                nc.gpsimd.tensor_tensor(shift[:, n, j, :], negmean[:, n, j, :], rstd[:, n, j, :],
                                        ALU.mult).then_inc(rstd_ready[n], 1)

            def project(j):
                s = j % 2
                pool.wait_ge(pos_l_ready, j + 1)
                nc.gpsimd.tensor_tensor(leaky_l[:, s, :], leaky_l[:, s, :], neg_l[:, s, :],
                                        ALU.subtract).then_inc(leaky_l_ready, 1)
                if j == 0:
                    pool.wait_ge(par_in, 16)
                    pool.wait_ge(con_in, 16)
                pool.wait_ge(h_in[j], 16)
                nc.gpsimd.tensor_tensor(h_beta[:, tiles(j), :], h_sb[:, tiles(j), :],
                                        views["beta"].unsqueeze(1).to_broadcast([P, TC, D]),
                                        ALU.add).then_inc(hbeta_ready, 1)

            def mix(j):
                rsqrt(0, j)

            def norm1(j):
                rsqrt(1, j)

            def dispatch(t):
                def scatter(j):
                    if t == 0:
                        pool.wait_ge(x1_low, j + 1)
                        pool.wait_ge(x1_high, j + 1)
                        pool.wait_ge(tags_ready, 1)
                        pool.wait_ge(slot_ready, j + 1)
                    for c in range(K2):
                        k = K2 * (TC * j + t) + c
                        nc.gpsimd.indirect_dma_start(x_rows[:, :],
                                                     bass.IndirectOffsetOnAxis(ap=slot[:, k:k + 1], axis=0),
                                                     x1_rows[:, TC * j + t, :], None).then_inc(dispatched, 16)
                return scatter

            in_order(project=project, mix=mix, norm1=norm1, dispatch0=dispatch(0), dispatch1=dispatch(1),
                     dispatch2=dispatch(2), dispatch3=dispatch(3))

            for q in range(Q):
                pool.wait_ge(yo_ready, q + 1)
                nc.gpsimd.indirect_dma_start(y_rows[:, :], bass.IndirectOffsetOnAxis(ap=dst[:, q:q + 1], axis=0),
                                             yo[:, q % DEPTH, :], None).then_inc(scattered[q % DEPTH], 16)

            def add_y1(j):
                pool.wait_ge(y1_scaled, j + 1)
                pool.wait_ge(y2_added, j + 1)
                nc.gpsimd.tensor_tensor(ya[:, tiles(j), :], ya[:, tiles(j), :], yb[:, tiles(j), :],
                                        ALU.add).then_inc(y1_added, 1)

            add_y1(0)
            add_y1(1)
            for j in range(2, NCH + 2):
                rsqrt(2, j - 2)
                if j < NCH:
                    add_y1(j)

        @block.vector
        def _(dve):
            links = [0]

            def link(ins):
                links[0] += 1
                ins.then_inc(dve_link, 1)
                dve.wait_ge(dve_link, links[0])

            dve.wait_ge(par0_in, 16)
            dve.wait_ge(con0_in, 16)
            nc.vector.tensor_scalar(att_r_blk[:, :], views["same_head"], views["att_r"], None, ALU.mult)
            nc.vector.tensor_scalar(att_l_blk[:, :], views["head_of"], views["att_l"], None,
                                    ALU.mult).then_inc(blocks_ready, 1)

            def project(j):
                s = j % 2
                dve.wait_ge(low_r_ready, j + 1)
                nc.vector.tensor_tensor(leaky_r[:, s, :], ps_fr[s][:, :], leaky_r[:, s, :],
                                        ALU.max).then_inc(leaky_r_ready, 1)
                if j == 0:
                    dve.wait_ge(con_in, 16)
                    nc.vector.tensor_copy(before_bf[:, :], views["before"]).then_inc(before_ready, 1)

            def scores(j):
                dve.wait_ge(sr_ready, j + 1)
                nc.vector.tensor_reduce(stat[:, j, 0:2], ps_sr[:, :].rearrange("p (b n) -> p b n", b=2), AX,
                                        ALU.max, negate=True).then_inc(negmax_ready, 1)

            def factors(j):
                s = j % 2
                for b in range(2):
                    dve.wait_ge(col_ready, 2 * j + b + 1)
                    ins = nc.vector.scalar_tensor_tensor(junk[:, b, :], col[:, s, b * N:(b + 1) * N], 1.0,
                                                         ps_fr[s][:, b * N:(b + 1) * N], ALU.mult, ALU.mult,
                                                         accum_out=csum[:, j, b:b + 1])
                link(ins)
                if j >= 2:
                    dve.wait_ge(g_ready, j - 1)
                nc.vector.tensor_tensor(csumd[:, s, :, :], views["head_of"].unsqueeze(1).to_broadcast([D, 2, H]),
                                        csum[:, j, :].unsqueeze(2).to_broadcast([D, 2, H]), ALU.mult)
                nc.vector.tensor_tensor(statd[:, s, :, :], views["head_first"].unsqueeze(1).to_broadcast([D, 4, H]),
                                        stat[:, j, :].unsqueeze(2).to_broadcast([D, 4, H]),
                                        ALU.mult).then_inc(csumd_ready, 1)

            def by_bank(a):
                return a[:, :].rearrange("p (e k) -> p e k", e=E)

            def quad(a):
                return a.rearrange("p (b u h) -> p b u h", b=2, u=2)

            def weigh(j):
                s = j % 2
                dve.wait_ge(sl_ready, j + 1)
                link(nc.vector.tensor_copy(stat_tok[:, s, :, :].rearrange("p k h -> p (k h)"), ps_stat))

                negr = stat_tok[:, s, 0:2, :].unsqueeze(2).to_broadcast([P, 2, 2, H])
                link(nc.vector.tensor_tensor(quad(rowmax[:, :]), quad(ps_sl), negr, ALU.subtract))
                link(nc.vector.tensor_tensor(d0[:, :], ps_sl, rowmax[:, :], ALU.subtract))
                nc.vector.tensor_tensor(quad(d1[:, :]), quad(d0[:, :]), negr, ALU.subtract).then_inc(d1_ready, 1)

            def scales(j):
                s = j % 2
                tot = stat_tok[:, s, 2:4, :].unsqueeze(2).to_broadcast([P, 2, 2, H])
                dve.wait_ge(row_ready, j + 1)
                link(nc.vector.tensor_tensor(quad(den[:, :]), quad(row[:, :]), tot, ALU.mult))
                link(nc.vector.reciprocal(rden[:, :], den[:, :]))
                nc.vector.tensor_tensor(scale[:, s, :, :].rearrange("p t h -> p (t h)"), row[:, :], rden[:, :],
                                        ALU.mult).then_inc(scale_ready, 1)

            def moments(n, x, j):
                for t in range(TC):
                    ins = nc.vector.bn_stats(bst[:, t, :], x[:, TC * j + t, :])
                link(ins)
                for t in range(TC):
                    ins = nc.vector.bn_aggr(mv[:, n, j, t, :], bst[:, t, :])
                link(ins)
                if n:
                    nc.vector.tensor_scalar(negmean[:, n, j, :], mv[:, n, j, :, 0], -1.0, None, ALU.mult)
                nc.vector.tensor_scalar(ve[:, n, j, :], mv[:, n, j, :, 1], LN_EPS, None,
                                        ALU.add).then_inc(mv_ready[n], 1)

            def mix(j):
                dve.wait_ge(h_in[j], 16)
                dve.wait_ge(fh_ready, j + 1)
                nc.vector.tensor_tensor(x1[:, tiles(j), :], by_tile(ps_mix), h_sb[:, tiles(j), :],
                                        ALU.add).then_inc(y_ready, 1)
                dve.wait_ge(y_ready, j + 1)
                moments(0, x1, j)
                if j == 0:
                    dve.wait_ge(par_in, 16)
                for t in range(TC):
                    ins = nc.vector.scalar_tensor_tensor(x1[:, TC * j + t, :], x1[:, TC * j + t, :],
                                                         mv[:, 0, j, t, 0:1], views["gamma"], ALU.subtract, ALU.mult)
                ins.then_inc(centred, 1)

            def norm1(j):
                dve.wait_ge(hbeta_ready, j + 1)
                dve.wait_ge(rstd_ready[0], j + 1)
                dve.wait_ge(centred, j + 1)
                for t in range(TC):
                    ins = nc.vector.scalar_tensor_tensor(x1[:, TC * j + t, :], x1[:, TC * j + t, :],
                                                         rstd[:, 0, j, t:t + 1], h_beta[:, TC * j + t, :],
                                                         ALU.mult, ALU.add)
                link(ins)
                moments(1, x1, j)

            def norm2(j):
                dve.wait_ge(rstd_ready[1], j + 1)
                for t in range(TC // 2):
                    ins = nc.vector.tensor_scalar(x1[:, TC * j + t, :], x1[:, TC * j + t, :], mv[:, 1, j, t, 0:1],
                                                  rstd[:, 1, j, t:t + 1], ALU.subtract, ALU.mult)
                ins.then_inc(x1_low, 1)

            def logits(j):
                T = tiles(j)
                dve.wait_ge(lg_ready, j + 1)
                link(nc.vector.tensor_tensor(lg[:, T, :], ps_lg.rearrange("p (t e) -> p t e", t=TC),
                                             views["gate_b"].unsqueeze(1).to_broadcast([P, TC, E]), ALU.add))
                for t in range(TC * j, TC * (j + 1)):
                    ins = nc.vector.max(top[:, t, :], lg[:, t, :])
                link(ins)
                for t in range(TC * j, TC * (j + 1)):
                    ins = nc.vector.max_index(topi[:, t, :], top[:, t, :], lg[:, t, :])
                link(ins)
                link(nc.vector.tensor_tensor(
                    pick[:, T, :, :], views["iota_e"].unsqueeze(1).unsqueeze(1).to_broadcast([P, TC, K2, E]),
                    topi[:, T, 0:K2].unsqueeze(3).to_broadcast([P, TC, K2, E]), ALU.is_equal))
                nc.vector.tensor_tensor(both[:, T, :], pick[:, T, 0, :], pick[:, T, 1, :],
                                        ALU.add).then_inc(both_ready, 1)
                nc.vector.tensor_tensor(exin[:, T, 0:E], lg[:, T, :], top[:, T, 0:1].to_broadcast([P, TC, E]),
                                        ALU.subtract)
                nc.vector.tensor_tensor(exin[:, T, E:E + 1], top[:, T, 1:2], top[:, T, 0:1],
                                        ALU.subtract).then_inc(exin_ready, 1)
                nc.vector.tensor_copy(x1_rows[:, T, D + 1:D + 2], topi[:, T, 0:1])

            def rank(j):
                T = tiles(j)
                T2 = slice(TC * K2 * j, TC * K2 * (j + 1))
                dve.wait_ge(rank_ready, j + 1)
                nc.vector.tensor_tensor(
                    rsel[:, :, :, :], pick[:, T, :, :],
                    ps_rank[:, 0:TC * E].rearrange("p (t e) -> p t e", t=TC).unsqueeze(2)
                    .to_broadcast([P, TC, K2, E]), ALU.mult).then_inc(rank_read, 1)
                dve.wait_ge(rank_read, j + 1)
                ranks = rankf[:, j % 2, :]
                link(nc.vector.tensor_reduce(ranks, rsel[:, :, :, :].rearrange("p t k e -> p (t k) e"), AX, ALU.add))
                nc.vector.scalar_tensor_tensor(slot[:, T2].rearrange("p (t k) -> p t k", k=K2), topi[:, T, 0:K2],
                                               float(REGION), ranks.rearrange("p (t k) -> p t k", k=K2),
                                               ALU.mult, ALU.add).then_inc(slot_ready, 1)
                if j == NCH - 1:
                    nc.vector.tensor_tensor(pads_at[:, :], ps_count[0:1, :], views["region"][0:1, :],
                                            ALU.add).then_inc(pads_at_ready, 1)
                    link(nc.vector.tensor_tensor(by_bank(cmp), by_bank(views["tile_floor"]),
                                                 ps_count.unsqueeze(2).to_broadcast([P, E, E]), ALU.is_lt))
                dve.wait_ge(exo_ready, j + 1)
                link(nc.vector.tensor_reduce(esum[:, T], exo[:, T, 0:E], AX, ALU.add))
                link(nc.vector.reciprocal(g12[:, T, 0], esum[:, T]))
                link(nc.vector.tensor_tensor(g12[:, T, 1], exo[:, T, E], g12[:, T, 0], ALU.mult))

            in_order(project=project, scores=scores, factors=factors, weigh=weigh, scales=scales, mix=mix, norm1=norm1,
                     norm2=norm2, logits=logits, rank=rank)

            link(nc.vector.tensor_reduce(ntl[:, :], by_bank(cmp), AX, ALU.add))
            link(nc.vector.tensor_tensor(by_bank(cmp), by_bank(views["bank_before"]),
                                         ntl[:, :].unsqueeze(1).to_broadcast([P, E, E]), ALU.mult))
            link(nc.vector.tensor_reduce(off[:, :], by_bank(cmp), AX, ALU.add))
            nc.vector.tensor_scalar(start[:, :], off[:, :], -1.0, None, ALU.mult)
            link(nc.vector.tensor_tensor(endt[:, :], off[:, :], ntl[:, :], ALU.add))
            nc.vector.tensor_tensor(start[:, :], start[:, :], views["start"], ALU.add)
            link(nc.vector.tensor_scalar(past[:, :], endt[:, :], views["tile"], None, ALU.is_le))
            link(nc.vector.scalar_tensor_tensor(within[:, :], off[:, :], views["tile"], past[:, :], ALU.is_le,
                                                ALU.subtract))
            nc.vector.scalar_tensor_tensor(junk_e[:, 0, :], start[:, :], 1.0, within[:, :], ALU.mult, ALU.mult,
                                           accum_out=row_bank[:, 0:1])
            nc.vector.scalar_tensor_tensor(junk_e[:, 1, :], views["iota_e"], 1.0, within[:, :], ALU.mult, ALU.mult,
                                           accum_out=row_bank[:, 1:2]).then_inc(row_bank_ready, 1)
            dve.wait_ge(tiles_turned, 1)
            nc.vector.tensor_scalar(tile_row[:, :], ps_tiles[0:1, 0:Q], float(E * REG_T), float(P), ALU.add, ALU.mult)
            nc.vector.tensor_copy(bank[:, 0:Q], ps_tiles[0:1, Q:2 * Q]).then_inc(tiles_ready, 1)

            nc.vector.tensor_copy(bank_hot[:, :], ps_tiles[0:E, 2 * Q:3 * Q]).then_inc(bank_hot_ready, 1)
            dve.wait_ge(by_q_summed, 1)
            nc.vector.tensor_copy(by_q[:, :, :].rearrange("p c q -> p (c q)"),
                                  ps_byq[:, 0:(FC + 1) * Q]).then_inc(by_q_ready, 1)
            link(nc.vector.tensor_tensor(gates[:, 0, :, :], pick[:, :, 0, :],
                                         g12[:, :, 0:1].to_broadcast([P, NT, E]), ALU.mult))
            link(nc.vector.tensor_tensor(gates[:, 1, :, :], pick[:, :, 1, :],
                                         g12[:, :, 1:2].to_broadcast([P, NT, E]), ALU.mult))
            nc.vector.tensor_tensor(gates[:, 0, :, :], gates[:, 0, :, :], gates[:, 1, :, :],
                                    ALU.add).then_inc(gates_ready, 1)
            dve.wait_ge(gates_turned, 1)
            nc.vector.tensor_copy(gates_t[:, :, :].rearrange("e j p -> e (j p)"),
                                  ps_gt[0:TC * E, :]).then_inc(gates_t_ready, 1)
            def copy_xt(q, k):
                dve.wait_ge(xt_done, q + 1)
                nc.vector.tensor_copy(xt[:, k % 2, :], ps_x[k % 2][:, 0:P]).then_inc(xt_copied, 1)

            def relu_low(q, k, c):
                if c == 0:
                    dve.wait_ge(up_low, q + 1)
                nc.vector.tensor_scalar(hid[:, k % 2, c, :], ps_h[k % 2][0][:, c * P:(c + 1) * P],
                                        by_q[:, c, bass.ds(q, 1)], 0.0, ALU.add, ALU.max).then_inc(relu_dve, 1)

            def copy_y(q, k, i):
                dve.wait_ge(down_done, q + 1)
                if not known(q) or q >= DEPTH:
                    dve.wait_ge(scattered[k], 16 * i)
                nc.vector.tensor_copy(yo[:, k, :], ps_y[k % 2][:, 0:D]).then_inc(yo_ready, 1)

            def index_parts(q, k, n=2):
                if not known(q) or q:
                    dve.wait_ge(dst_ready, q)
                tag = xg[:, k:k + n, :]
                nc.vector.tensor_tensor(first[:, 0:n], tag[:, :, D + 1], by_q[:, FC, bass.ds(q, n)], ALU.is_equal)
                nc.vector.tensor_tensor(dump[:, 0:n], tag[:, :, D + 2], views["dump"][:, bass.ds(q, n)],
                                        ALU.mult).then_inc(parts_link, n)

            def index_rows(q, k, n=2):
                dve.wait_ge(parts_link, q + n)
                nc.vector.scalar_tensor_tensor(row_no[:, 0:n], first[:, 0:n], float(TOK), xg[:, k:k + n, D],
                                               ALU.mult, ALU.add).then_inc(row_no_link, n)

            def index(q, k, n=2):
                dve.wait_ge(row_no_link, q + n)
                nc.vector.tensor_tensor(dst[:, bass.ds(q, n)], row_no[:, 0:n], dump[:, 0:n],
                                        ALU.add).then_inc(dst_ready, n)

            copy_xt(0, 0)
            copy_xt(1, 1)
            relu_low(0, 0, 0)
            relu_low(0, 0, 1)
            index_parts(0, 0)
            index_rows(0, 0)
            index(0, 0)

            def step(q, k, i):
                if not known(q) or q + 2 < Q:
                    copy_xt(q + 2, k + 2)
                more = not known(q) or q + 1 < Q
                n = 2 if not known(q) or q + 2 < Q else 1
                if k % 2:
                    index_parts(q + 1, (k + 1) % DEPTH, n)
                if more:
                    relu_low(q + 1, k + 1, 0)
                if k % 2:
                    index_rows(q + 1, (k + 1) % DEPTH, n)
                if more:
                    relu_low(q + 1, k + 1, 1)
                if k % 2:
                    index(q + 1, (k + 1) % DEPTH, n)
                copy_y(q, k, i)

            loop(dve, step)

            for j in range(NCH):
                dve.wait_ge(bias_ready, j + 1)
                nc.vector.tensor_tensor(base[:, tiles(j), :], by_tile(ps_bias[j % 2]), x1[:, tiles(j), :],
                                        ALU.add).then_inc(base_ready, 1)

            def add_y2(j):
                dve.wait_ge(yb_in[j], 16)
                for t in range(TC * j, TC * (j + 1)):
                    ins = nc.vector.scalar_tensor_tensor(yb[:, t, :], yb[:, t, :], g12[:, t, 1:2], base[:, t, :],
                                                         ALU.mult, ALU.add)
                ins.then_inc(y2_added, 1)

            def last_moments(j):
                dve.wait_ge(y1_added, j + 1)
                moments(2, ya, j)

            dve.wait_ge(base_ready, NCH)
            add_y2(0)
            add_y2(1)
            for j in range(2, NCH + 2):
                last_moments(j - 2)
                if j < NCH:
                    add_y2(j)
            for j in range(NCH - 2, NCH):
                dve.wait_ge(rstd_ready[2], j + 1)
                for t in range(TC // 2):
                    ins = nc.vector.tensor_scalar(res[:, TC * j + t, :], ya[:, TC * j + t, :], mv[:, 2, j, t, 0:1],
                                                  rstd[:, 2, j, t:t + 1], ALU.subtract, ALU.mult)
                ins.then_inc(last_halves, 1)

        @block.tensor
        def _(pe):
            ident = views["ident"]

            def project(j):
                s = j % 2
                if j == 0:
                    pe.wait_ge(par0_in, 16)
                pe.wait_ge(ht_in[j], 16)
                rows = ht_sb[:, j * CW:(j + 1) * CW]
                if j >= 2:
                    pe.wait_ge(csumd_ready, j - 1)
                nc.tensor.matmul(ps_fr[s][:, :], views["wr_t"], rows, start=True, stop=True).then_inc(fr_ready, 1)
                if j:
                    pe.wait_ge(pos_l_ready, j)
                nc.tensor.matmul(ps_fl[:, :], views["wl_t"], rows, start=True, stop=True).then_inc(fl_ready, 1)

            def scores(j):
                if j == 0:
                    pe.wait_ge(blocks_ready, 1)
                else:
                    pe.wait_ge(col_ready, 2 * j)
                pe.wait_ge(leaky_r_ready, j + 1)
                nc.tensor.matmul(ps_sr[:, :], att_r_blk[:, :], leaky_r[:, j % 2, :], start=True,
                                 stop=True).then_inc(sr_ready, 1)

            def weigh(j):
                s = j % 2
                if j == 0:
                    pe.wait_ge(ones_ready, 1)
                    pe.wait_ge(par_in, 16)
                else:
                    pe.wait_ge(d1_ready, j)
                    pe.wait_ge(g_copied, j)
                pe.wait_ge(leaky_l_ready, j + 1)
                for t in range(TC):
                    nc.tensor.matmul(ps_sl[:, H * t:H * (t + 1)], leaky_l[:, s, t * P:(t + 1) * P],
                                     att_l_blk[:, :], start=True, stop=True)
                pe.wait_ge(csumd_ready, j + 1)
                nc.tensor.matmul(ps_stat, ones[:, :], statd[:, s, :, :].rearrange("p k h -> p (k h)"), start=True,
                                 stop=True).then_inc(sl_ready, 1)
                for b in range(2):
                    ins = nc.tensor.matmul(ps_g[0:H, b * D:(b + 1) * D], csumd[:, s, b, :], views["wf_t"],
                                           start=True, stop=True)
                ins.then_inc(g_ready, 1)

            def turn(j):
                s = j % 2
                if j == 0:
                    pe.wait_ge(con_in, 16)
                else:
                    pe.wait_ge(y_ready, j)
                pe.wait_ge(scale_ready, j + 1)
                for t in range(TC):
                    ins = nc.tensor.transpose(ps_mix[0:H, t * P:(t + 1) * P], scale[:, s, t, :], ident)
                ins.then_inc(scale_t_ready, 1)

            def mix(j):
                s = j % 2
                pe.wait_ge(g_copied, j + 1)
                pe.wait_ge(scale_t_copied, j + 1)
                for t in range(TC):
                    ins = nc.tensor.matmul(ps_mix[:, t * P:(t + 1) * P], scale_t[:, s, t * P:(t + 1) * P],
                                           g_sb[:, s, t // 2, :], start=True, stop=True)
                ins.then_inc(fh_ready, 1)

            def turn_x1(j):
                if j:
                    pe.wait_ge(rank_read, j)
                pe.wait_ge(x1_low, j + 1)
                pe.wait_ge(x1_high, j + 1)
                for t in range(TC):
                    ins = nc.tensor.transpose(ps_rt[:, t * P:(t + 1) * P], x1[:, TC * j + t, :], ident)
                ins.then_inc(x1t_ready, 1)

            def logits(j):
                pe.wait_ge(x1t_copied, j + 1)
                for t in range(TC):
                    ins = nc.tensor.matmul(ps_lg[:, E * t:E * (t + 1)], x1t[:, j % 2, t * P:(t + 1) * P],
                                           views["gate_w"], start=True, stop=True)
                ins.then_inc(lg_ready, 1)

            def rank(j):
                if j == 0:
                    pe.wait_ge(before_ready, 1)
                pe.wait_ge(both_ready, j + 1)
                for t in range(TC * (j + 1)):
                    lo = max(t - TC * j + 1, 0)
                    nc.tensor.matmul(ps_rank[:, E * lo:E * (TC + 1)], ones_bf[:, :],
                                     both[:, t, :].unsqueeze(1).to_broadcast([P, TC + 1 - lo, E]),
                                     start=t == 0, stop=False, skip_group_check=True)
                for t in range(TC):
                    ins = nc.tensor.matmul(ps_rank[:, E * t:E * (t + 1)], before_bf[:, :], both[:, TC * j + t, :],
                                           start=False, stop=t == TC - 1, skip_group_check=True)
                ins.then_inc(rank_ready, 1)

            in_order(project=project, scores=scores, weigh=weigh, turn=turn, mix=mix, turn_x1=turn_x1, logits=logits,
                     rank=rank)

            pe.wait_ge(row_bank_ready, 1)
            for c in range(2):
                ins = nc.tensor.matmul(ps_tiles[0:1, c * Q:(c + 1) * Q], row_bank[:, c:c + 1], ident[:, 0:Q],
                                       start=True, stop=True)
            ins = nc.tensor.transpose(ps_tiles[0:E, 2 * Q:2 * Q + P], within[:, :], ident)
            ins.then_inc(tiles_turned, 1)
            pe.wait_ge(b_in, 16 * (1 + TC))
            pe.wait_ge(bank_hot_ready, 1)
            for c in range(FC + 1):
                which = b1_sb[:, c * P:(c + 1) * P] if c < FC else views["bank_no"][0:E, :]
                ins = nc.tensor.matmul(ps_byq[:, c * Q:(c + 1) * Q], which, bank_hot[:, :], start=True, stop=True)
            ins.then_inc(by_q_summed, 1)
            pe.wait_ge(gates_ready, 1)
            for j in range(NCH):
                ins = nc.tensor.transpose(ps_gt[0:TC * E, j * P:(j + 1) * P],
                                          gates[:, 0, tiles(j), :].rearrange("p t e -> p (t e)"), ident)
            ins.then_inc(gates_turned, 1)

            held = [pe.alloc_register(f"pe_bank{k}") for k in range(2)]

            def turn_x(q, k, i):
                pe.wait_ge(x_in[k % DEPTH], 16 * (i + 1))
                nc.tensor.transpose(ps_x[k % 2][:, 0:P], xg[:, k % DEPTH, 0:D], ident).then_inc(xt_done, 1)

            def up(q, k):
                pe.wait_ge(xt_copied, q + 1)
                pe.wait_ge(w1_ready, q + 1)
                for c in range(FC):
                    half = c // 2
                    ins = nc.tensor.matmul(ps_h[k % 2][half][:, (c % 2) * P:(c % 2 + 1) * P],
                                           w1_now[:, k % 2, c * P:(c + 1) * P], xt[:, k % 2, :], start=True,
                                           stop=True)
                    if c % 2:
                        ins.then_inc((up_low, up_high)[half], 1)

            def down(q, k):
                e = pe.snap(held[k % 2], min_val=0, max_val=E - 1)
                pe.wait_ge(relu_dve, 2 * (q + 1))
                for c in range(FC):
                    if c == FC // 2:
                        pe.wait_ge(relu_act, q + 1)
                    ins = nc.tensor.matmul(ps_y[k % 2][:, 0:D], hid[:, k % 2, c, :],
                                           w2_sb[:, bass.ds(e * F + c * P, P)], start=c == 0, stop=c == FC - 1)
                ins.then_inc(down_done, 1)

            pe.wait_ge(w_in, 16 * E // 2)
            pe.wait_ge(tiles_ready, 1)
            turn_x(0, 0, 0)
            turn_x(1, 1, 0)
            up(0, 0)

            def step(q, k, i):
                if not known(q) or q + 2 < Q:
                    turn_x(q + 2, k + 2, i + (k + 2) // DEPTH)
                if not known(q) or q + 1 < Q:
                    up(q + 1, k + 1)
                pe.reg_load(held[k % 2], bank[0:1, bass.ds(q, 1)])
                down(q, k)

            loop(pe, step)

            pe.wait_ge(gates_t_ready, 1)
            for j in range(NCH):
                if j >= 2:
                    pe.wait_ge(base_ready, j - 1)
                nc.tensor.matmul(ps_bias[j % 2][:, :], gates_t[:, j, :], b2_sb[:, :, :].rearrange("e t d -> e (t d)"),
                                 start=True, stop=True).then_inc(bias_ready, 1)


def kernel(L0_attn_h, L0_attn_Wl, L0_attn_Wr, L0_attn_att_l, L0_attn_att_r, L0_attn_Wf, L0_attn_ln_gamma,
           L0_attn_ln_beta, L0_ffn_Wr, L0_ffn_br, L0_ffn_W1, L0_ffn_b1, L0_ffn_W2, L0_ffn_b2):
    import concourse.bacc as bacc
    from concourse.bass_utils import run_bass_kernel_spmd

    a = [np.asarray(x) for x in (L0_attn_h, L0_attn_Wl, L0_attn_Wr, L0_attn_att_l, L0_attn_att_r, L0_attn_Wf,
                                 L0_attn_ln_gamma, L0_attn_ln_beta, L0_ffn_Wr, L0_ffn_br, L0_ffn_W1, L0_ffn_b1,
                                 L0_ffn_W2, L0_ffn_b2)]
    h, wl, wr, att_l, att_r, wf, gamma, beta, gw, gb, w1, b1, w2, b2 = a

    def rows(v):
        return np.broadcast_to(v.reshape(1, -1), (P, v.size))

    c0, c = shape_constants()
    ins = {
        "h": h,
        "h_t": h.reshape(B, P, 2, D).transpose(3, 0, 2, 1).reshape(D, TOK),
        "first_params": np.concatenate([wr.T, wl.T, np.tile(att_r.reshape(-1), H)[:, None],
                                        np.tile(att_l.reshape(-1), H)[:, None]], axis=1),
        "params": np.concatenate([wf.T, rows(gamma), rows(beta), gw, rows(gb)], axis=1),
        "first_consts": c0,
        "consts": c,
        "w1": w1.transpose(1, 0, 2).reshape(D, E * F),
        "w2": w2.reshape(E, FC, P, D).transpose(2, 0, 1, 3).reshape(P, E * F),
        "b1": b1.reshape(E, F),
        "b2": b2.reshape(E, D),
    }
    ins = {k: np.ascontiguousarray(v) for k, v in ins.items()}
    nc = bacc.Bacc("TRN2", target_bir_lowering=False, num_devices=1)
    aps = [nc.dram_tensor(k, v.shape, mybir.dt.from_np(v.dtype), kind="ExternalInput").ap() for k, v in ins.items()]
    out = nc.dram_tensor("out", (B, N, D), mybir.dt.float32, kind="ExternalOutput").ap()
    x_rows = nc.dram_tensor("x_rows", (XROWS, W), mybir.dt.float32, kind="Internal").ap()
    y_rows = nc.dram_tensor("y_rows", (YROWS, D), mybir.dt.float32, kind="Internal").ap()
    routed_block(nc, *aps, out, x_rows, y_rows)
    r = run_bass_kernel_spmd(nc, [ins], core_ids=[0])
    return r.results[0]["out"]
```
